# Optimizing a Trainium2 kernel written in Bass

```python
import numpy as np
import jax
import jax.numpy as jnp

def _softmax(x, axis=-1):
    return jax.nn.softmax(x, axis=axis)

def _gelu(x):
    return jax.nn.gelu(x, approximate=True)

def _silu(x):
    return jax.nn.silu(x)

def _sigmoid(x):
    return jax.nn.sigmoid(x)

def _layernorm(x, axis=-1, eps=1e-05):
    m = jnp.mean(x, axis=axis, keepdims=True)
    v = jnp.var(x, axis=axis, keepdims=True)
    return (x - m) / jnp.sqrt(v + eps)

def _scatter_add(tgt, idx, src, axis=0):
    return tgt.at[idx].add(src)

def _segment_sum(src, seg, n):
    return jax.ops.segment_sum(src, seg, n)
kernel_name = 'mk_seq_preln_d1_jaxref_r8_ab4b14'

def setup_inputs(seed: int=0):
    np.random.seed(seed)
    _w = jnp.asarray

    def _L0_attn_setup():
        import jax, jax.numpy as jnp
        import numpy as np
        D_MODEL = 128
        N_HEADS = 16
        HEAD_DIM = D_MODEL // N_HEADS
        D_LATENT = 32
        LAMBDA_DECAY = 0.01
        TIME_STEP = 0.01
        CLAMP = 10000.0

        def _reference_tuple_inner(x, Wq, Wk, Wv, Wo, W_down_kv, W_up_k, W_up_v):
            B, S, _ = x.shape
            q = x @ Wq
            k = x @ Wk
            v = x @ Wv
            latent_kv = (k + v) @ W_down_kv
            k_rec = latent_kv @ W_up_k
            v_rec = latent_kv @ W_up_v

            def heads(t):
                return t.reshape(B, S, N_HEADS, HEAD_DIM).transpose(0, 2, 1, 3)
            qh, kh, vh = (heads(q), heads(k_rec), heads(v_rec))
            scale = 1.0 / (jnp.sqrt(jnp.float32(D_MODEL)) + 1e-08)
            scores = jnp.einsum('bhqd,bhkd->bhqk', qh, kh) * scale
            scores = jnp.clip(jnp.nan_to_num(scores, nan=-1000000000.0), -CLAMP, CLAMP)
            idx = jnp.arange(S, dtype=jnp.float32)
            decay = jnp.exp(-LAMBDA_DECAY * TIME_STEP * jnp.abs(idx[:, None] - idx[None, :]))
            scores = scores * decay[None, None, :, :]
            scores = jnp.clip(jnp.nan_to_num(scores, nan=-1000000000.0), -CLAMP, CLAMP)
            attn = jax.nn.softmax(scores, axis=-1)
            out = jnp.einsum('bhqk,bhkd->bhqd', attn, vh)
            out = out.transpose(0, 2, 1, 3).reshape(B, S, D_MODEL)
            return (out @ Wo, latent_kv)
        key = jax.random.key(seed)
        ks = jax.random.split(key, 8)
        B, S = (2, 256)

        def w(k, i, o):
            return jax.random.normal(k, (i, o), dtype=jnp.float32) * 0.02
        return {'x': jax.random.normal(ks[0], (B, S, D_MODEL), dtype=jnp.float32), 'Wq': w(ks[1], D_MODEL, D_MODEL), 'Wk': w(ks[2], D_MODEL, D_MODEL), 'Wv': w(ks[3], D_MODEL, D_MODEL), 'Wo': w(ks[4], D_MODEL, D_MODEL), 'W_down_kv': w(ks[5], D_MODEL, D_LATENT), 'W_up_k': w(ks[6], D_LATENT, D_MODEL), 'W_up_v': w(ks[7], D_LATENT, D_MODEL)}
    _L0_attn_in = _L0_attn_setup()

    def _L0_ffn_setup():
        import jax, jax.numpy as jnp
        import numpy as np
        FEATURES = 128
        D_IN = 128

        def fp8_gemm_optimized(x, input_scale, kernel, kernel_scale):
            s_in = input_scale[0]
            s_k = kernel_scale[0]
            x_q = (x.astype(jnp.float32) / s_in).astype(jnp.float8_e4m3fn)
            k_q = (kernel.astype(jnp.float32) / s_k).astype(jnp.float8_e4m3fn)
            y = jnp.dot(x_q.astype(jnp.float32), k_q.astype(jnp.float32), preferred_element_type=jnp.float32)
            return y * (s_in * s_k)
        key = jax.random.key(seed)
        kx, kk, kb = jax.random.split(key, 3)
        x = jax.random.normal(kx, (4, 1024, D_IN), dtype=jnp.float32)
        limit = np.sqrt(6.0 / (D_IN + FEATURES)).astype(np.float32)
        kernel = jax.random.uniform(kk, (D_IN, FEATURES), dtype=jnp.float32, minval=-limit, maxval=limit).astype(jnp.bfloat16)
        input_scale = jnp.ones((1,), dtype=jnp.float32)
        kernel_scale = jnp.ones((1,), dtype=jnp.float32)
        bias = jnp.zeros((FEATURES,), dtype=jnp.bfloat16)
        return {'x': x, 'kernel': kernel, 'input_scale': input_scale, 'kernel_scale': kernel_scale, 'bias': bias}
    _L0_ffn_in = _L0_ffn_setup()
    _d = {'L0_attn_x': _L0_attn_in['x'], 'L0_attn_Wq': _L0_attn_in['Wq'], 'L0_attn_Wk': _L0_attn_in['Wk'], 'L0_attn_Wv': _L0_attn_in['Wv'], 'L0_attn_Wo': _L0_attn_in['Wo'], 'L0_attn_W_down_kv': _L0_attn_in['W_down_kv'], 'L0_attn_W_up_k': _L0_attn_in['W_up_k'], 'L0_attn_W_up_v': _L0_attn_in['W_up_v'], 'L0_ffn_kernel': _L0_ffn_in['kernel'], 'L0_ffn_input_scale': _L0_ffn_in['input_scale'], 'L0_ffn_kernel_scale': _L0_ffn_in['kernel_scale'], 'L0_ffn_bias': _L0_ffn_in['bias']}
    _x0 = _d['L0_attn_x']
    _d['L0_attn_x'] = jax.random.normal(jax.random.fold_in(jax.random.key(seed), 1), (4, 1024, 128), dtype=_x0.dtype)
    del _x0
    return _d

def reference(L0_attn_x, L0_attn_Wq, L0_attn_Wk, L0_attn_Wv, L0_attn_Wo, L0_attn_W_down_kv, L0_attn_W_up_k, L0_attn_W_up_v, L0_ffn_kernel, L0_ffn_input_scale, L0_ffn_kernel_scale, L0_ffn_bias):

    def _L0_attn_ref(x, Wq, Wk, Wv, Wo, W_down_kv, W_up_k, W_up_v):
        import jax, jax.numpy as jnp
        import numpy as np
        D_MODEL = 128
        N_HEADS = 16
        HEAD_DIM = D_MODEL // N_HEADS
        D_LATENT = 32
        LAMBDA_DECAY = 0.01
        TIME_STEP = 0.01
        CLAMP = 10000.0

        def _reference_tuple_inner(x, Wq, Wk, Wv, Wo, W_down_kv, W_up_k, W_up_v):
            B, S, _ = x.shape
            q = x @ Wq
            k = x @ Wk
            v = x @ Wv
            latent_kv = (k + v) @ W_down_kv
            k_rec = latent_kv @ W_up_k
            v_rec = latent_kv @ W_up_v

            def heads(t):
                return t.reshape(B, S, N_HEADS, HEAD_DIM).transpose(0, 2, 1, 3)
            qh, kh, vh = (heads(q), heads(k_rec), heads(v_rec))
            scale = 1.0 / (jnp.sqrt(jnp.float32(D_MODEL)) + 1e-08)
            scores = jnp.einsum('bhqd,bhkd->bhqk', qh, kh) * scale
            scores = jnp.clip(jnp.nan_to_num(scores, nan=-1000000000.0), -CLAMP, CLAMP)
            idx = jnp.arange(S, dtype=jnp.float32)
            decay = jnp.exp(-LAMBDA_DECAY * TIME_STEP * jnp.abs(idx[:, None] - idx[None, :]))
            scores = scores * decay[None, None, :, :]
            scores = jnp.clip(jnp.nan_to_num(scores, nan=-1000000000.0), -CLAMP, CLAMP)
            attn = jax.nn.softmax(scores, axis=-1)
            out = jnp.einsum('bhqk,bhkd->bhqd', attn, vh)
            out = out.transpose(0, 2, 1, 3).reshape(B, S, D_MODEL)
            return (out @ Wo, latent_kv)
        return _reference_tuple_inner(x, Wq, Wk, Wv, Wo, W_down_kv, W_up_k, W_up_v)[0]

    def _L0_ffn_ref(x, kernel, input_scale, kernel_scale, bias):
        import jax, jax.numpy as jnp
        import numpy as np
        FEATURES = 128
        D_IN = 128

        def fp8_gemm_optimized(x, input_scale, kernel, kernel_scale):
            s_in = input_scale[0]
            s_k = kernel_scale[0]
            x_q = (x.astype(jnp.float32) / s_in).astype(jnp.float8_e4m3fn)
            k_q = (kernel.astype(jnp.float32) / s_k).astype(jnp.float8_e4m3fn)
            y = jnp.dot(x_q.astype(jnp.float32), k_q.astype(jnp.float32), preferred_element_type=jnp.float32)
            return y * (s_in * s_k)
        dtype = jnp.bfloat16
        x = x.astype(dtype)
        orig_shape = x.shape
        x2 = x.reshape(-1, x.shape[-1])
        y = fp8_gemm_optimized(x2, input_scale, kernel, kernel_scale)
        y = y.astype(dtype) + bias
        return y.reshape(orig_shape[:-1] + (FEATURES,))
    x = L0_attn_x
    x = x + _L0_attn_ref(_layernorm(x, axis=-1), L0_attn_Wq, L0_attn_Wk, L0_attn_Wv, L0_attn_Wo, L0_attn_W_down_kv, L0_attn_W_up_k, L0_attn_W_up_v)
    x = x + _L0_ffn_ref(_layernorm(x, axis=-1), L0_ffn_kernel, L0_ffn_input_scale, L0_ffn_kernel_scale, L0_ffn_bias)
    return x

_drawn_inputs = setup_inputs


def setup_inputs(seed=0):
    import zlib

    import numpy as np

    out = dict(_drawn_inputs(seed))
    spreads = {'L0_ffn_bias': (0.0, 0.268)}
    factors = {'L0_attn_Wq': 8.0,
     'L0_attn_Wk': 8.0,
     'L0_attn_Wv': 8.0,
     'L0_attn_Wo': 8.0,
     'L0_attn_W_down_kv': 8.0,
     'L0_attn_W_up_k': 8.0,
     'L0_attn_W_up_v': 8.0}
    for name, (base, spread) in spreads.items():
        noise = np.random.default_rng([zlib.crc32(name.encode()), seed]).standard_normal(out[name].shape)
        drawn = base * np.exp(spread * noise) if base else spread * noise
        out[name] = jnp.asarray(drawn.astype(out[name].dtype))
    for name, factor in factors.items():
        out[name] = (out[name] * factor).astype(out[name].dtype)
    return out
```

```python
import concourse.bass as bass
from concourse import mybir
from contextlib import ExitStack

F32 = mybir.dt.float32
BF16 = mybir.dt.bfloat16
I32 = mybir.dt.int32
ALU = mybir.AluOpType
ACT = mybir.ActivationFunctionType
AX = mybir.AxisListType

B, S, D = 4, 1024, 128
H, HD = 16, 8
DL = 32
P = 128
NT = B * S // P
NB = S // P
HG = 4
G = H // HG
CH = 512
NC = B * S // CH
PARTS = 3
ROWS = HD * PARTS * PARTS
KROWS = 96
VW = HD + 1
FILL = 16 * 2 * PARTS * HG
SCALE = 1.0 / (float(D) ** 0.5 + 1e-8)
CLAMP = 10000.0
EPS = 1e-5
SCORE_BOUND = 40.0
VALUE_BOUND = 1e16
NORM_LIMIT = (SCORE_BOUND / SCALE) ** 2 / 1.02
Q, K = range(2)
PLUS, MINUS = range(2)
NAN_SCALE = 3.0e38 / (464.0 * 464.0)
TABLE = 2 * S - P
RSQRT_MAGIC = float(0x5F3759DF)

JOBS = [("T", 0)]
for _c in range(NC):
    JOBS += [("T", _c + 1)] * (_c + 1 < NC) + [("q", _c), ("k", _c), ("v", _c)]


def build(nc, x, wq, wk, wv, wo, wd, wuk, wuv, w8, s_in, s_k, bias, decay_rows, decay_table,
          diag_fix, ident, head_sum, out, qt_dram, kt_dram, rec_dram):
    with ExitStack() as ctx:
        def sb(name, shape, dt=F32):
            return ctx.enter_context(nc.sbuf_tensor(name, shape, dt))

        def sem(name):
            return ctx.enter_context(nc.semaphore(name))

        qT = sb("qT", [P, B * S])
        kT = sb("kT", [P, B * S])
        V = sb("V", [P, NT, H, VW])
        Vb = sb("Vb", [P, NB, H, VW])
        stage = sb("stage", [P, 2, HG, 2, 2, S], BF16)
        probs = sb("probs", [P, 2 * HG, S])
        parts = sb("parts", [P, 2, PARTS, 2, S], BF16)
        pv_out = sb("pv_out", [P, S])
        o_raw = sb("o_raw", [P, S])
        den = sb("den", [P, S // HD])
        rec = sb("rec", [P, S // HD])
        rec_b = sb("rec_b", [P, S])
        decay = sb("decay", [P, 2, S])
        split_s = sb("split_s", [P, S])
        fix = sb("fix", [P, P])
        eye = sb("eye", [P, P])
        eye16 = sb("eye16", [P, P], BF16)
        hsum = sb("hsum", [P, 32], BF16)
        wq_s = sb("wq_s", [P, D])
        wo_s = sb("wo_s", [P, D])
        wk_eff = sb("wk_eff", [P, D])
        wv_eff = sb("wv_eff", [P, D])
        w8_s = sb("w8_s", [P, D], BF16)
        kq = sb("kq", [P, D], BF16)
        bias_s = sb("bias_s", [P, D], BF16)
        scales = sb("scales", [P, 2])
        rscales = sb("rscales", [P, 2])
        oscale = sb("oscale", [P, 1])
        stats = sb("stats", [P, NT, 6])
        mv = sb("mv", [P, NT, 2])
        rs = sb("rs", [P, 3, NT])
        norms = sb("norms", [P, 8])
        flag = sb("flag", [1, 1], I32)
        ones = sb("ones", [P, 1])

        X = probs[:, 0:HG, :].rearrange("p a (t d) -> p (a t) d", d=D)
        xnT = probs[:, HG:2 * HG, :].rearrange("p a n -> p (a n)")
        parts_flat = parts[:, :, :, :, :].rearrange("p a k v n -> p (a k v n)")
        squares = parts_flat[:, 0:2 * B * S]
        wk_s, wv_s, wkv_T = [pv_out[:, i * D:(i + 1) * D] for i in range(3)]
        wuk_s, wuv_s, wdown_T = [pv_out[0:DL, i * D:(i + 1) * D] for i in range(3, 6)]
        w8f, w8m = [split_s[:, i * D:(i + 1) * D] for i in range(2)]
        wd_s, hsum_f = [split_s[:, 2 * D + i * DL:2 * D + (i + 1) * DL] for i in range(2)]
        OT = qT
        gen = stage[:, :, :, :, :, :].rearrange("p u j a v n -> p (u j a v n)").bitcast(F32)
        g_clip, g_dec_s, g_p, g_pT_s = [gen[:, i * S:(i + 1) * S] for i in range(4)]
        g_otok = gen[:, 4 * S:8 * S]
        g_table_s = gen[:, 8 * S:8 * S + TABLE]
        g_q, g_k = gen[0:HD, 10 * S:11 * S], gen[0:HD, 11 * S:12 * S]

        ps = ctx.enter_context(nc.psum_tensor("ps", [P, 8, CH], F32))
        ps_all = ps[:, :, :].rearrange("p b n -> p (b n)")
        score = [ps_all[:, 0:S], ps_all[:, S:2 * S]]
        pv = ps_all[:, 6 * CH:8 * CH]

        x_in = [sem(f"x_in{b}") for b in range(B)]
        w_in = sem("w_in")
        c_in = sem("c_in")
        waited = sem("waited")
        const_in = sem("const_in")
        kq_ready = sem("kq_ready")
        pv_clear = sem("pv_clear")
        g_ot = sem("g_ot")
        dve_step = sem("dve_step")
        split_step = sem("split_step")
        pool_split = sem("pool_split")
        pool_tail = sem("pool_tail")
        wkv_ready = sem("wkv_ready")
        fold_pe = sem("fold_pe")
        fold_act = sem("fold_act")
        xn_ready = sem("xn_ready")
        tr_ready = sem("tr_ready")
        xnT_ready = sem("xnT_ready")
        q_ps = sem("q_ps")
        k_ps = sem("k_ps")
        v_ps = sem("v_ps")
        q_sb = sem("q_sb")
        k_sb = sem("k_sb")
        v_sb = sem("v_sb")
        sq_ready = sem("sq_ready")
        norm_ps = sem("norm_ps")
        ok_ready = sem("ok_ready")
        ok_ps = sem("ok_ps")
        flag_ready = sem("flag_ready")
        pads_zero = sem("pads_zero")
        const_ready = sem("const_ready")
        parts_ready = sem("parts_ready")
        vb_ready = sem("vb_ready")
        stage_in = [sem(f"stage_in{u}") for u in range(2)]
        edge_ready = sem("edge_ready")
        diag_fixed = sem("diag_fixed")
        qk_done = sem("qk_done")
        exp_done = sem("exp_done")
        pv_done = sem("pv_done")
        pv_copied = sem("pv_copied")
        out_moved = sem("out_moved")
        rec_ready = sem("rec_ready")
        rec_stored = sem("rec_stored")
        rec_in = sem("rec_in")
        ot_ready = sem("ot_ready")
        g_dram = sem("g_dram")
        g_table = sem("g_table")
        g_in = sem("g_in")
        g_step = sem("g_step")
        g_init = sem("g_init")
        g_scores = sem("g_scores")
        g_scores_free = sem("g_scores_free")
        g_max = sem("g_max")
        g_exp = sem("g_exp")
        g_tr = sem("g_tr")
        g_pT = sem("g_pT")
        g_o = sem("g_o")
        g_norm = sem("g_norm")
        g_otr = sem("g_otr")
        x2_in = [sem(f"x2_in{b}") for b in range(B)]
        proj_ps = sem("proj_ps")
        x1_ready = sem("x1_ready")
        ln2_ready = sem("ln2_ready")
        scaled = sem("scaled")
        magic_ready = sem("magic_ready")
        rounded = sem("rounded")
        xq_ready = sem("xq_ready")
        xqT_ps = sem("xqT_ps")
        xqT_ready = sem("xqT_ready")
        y_ps = sem("y_ps")
        y_ready = sem("y_ready")
        y_free = sem("y_free")
        res_ready = sem("res_ready")
        stored = sem("stored")

        block = ctx.enter_context(nc.Block())

        X1 = X
        tailb = parts_flat
        xn2 = tailb[:, 0:S]
        xq = tailb[:, S:2 * S]
        xqT = tailb[:, 2 * S:3 * S]
        yb = tailb[:, 3 * S:4 * S]
        xs = tailb[:, 4 * S:6 * S].bitcast(F32)
        magic = tailb[:, 6 * S:8 * S].bitcast(F32)
        rnd = tailb[:, 8 * S:10 * S].bitcast(F32)
        res = probs[:, HG:2 * HG, :]
        proj = score
        xqT_b = ps[:, 4, :].bitcast(BF16)
        yps = ps_all[:, 6 * CH:8 * CH]

        def wait(engine, semaphore, value):
            engine.wait_ge(semaphore, value)
            engine.sem_inc(waited, 1)

        @block.sync
        def _(sp):
            x_t = x.rearrange("(t p) d -> p t d", p=P)
            for b in range(B):
                sp.dma_start(X[:, b * NB:(b + 1) * NB, :], x_t[:, b * NB:(b + 1) * NB, :]).then_inc(x_in[b], 16)
            sp.dma_start(decay[:, :, :].rearrange("p a n -> p (a n)"),
                         decay_rows.broadcast_to([P, 2 * S])).then_inc(c_in, 16)
            sp.dma_start(fix[:, :], diag_fix[:, :]).then_inc(c_in, 16)

            sp.wait_ge(flag_ready, 1)
            bounded = sp.value_load(flag[0:1, 0:1], min_val=0, max_val=1)
            with sp.If(bounded > 0):
                def stage_group(b, hg, u):
                    if not (isinstance(b, int) and b == 0 and hg < 2):
                        wait(sp, qk_done, HG * NB * (b * G + hg - 1))
                    for j in range(HG):
                        h = hg * HG + j
                        for part in range(PARTS):
                            rows = slice(part, ROWS, PARTS)
                            q_parts = parts[HD * h:HD * h + HD, Q, :, :, :].rearrange("p k v n -> p k (v n)")
                            k_part = parts[HD * h:HD * h + HD, K, part, :, :].rearrange("p (o v) n -> p o (v n)", o=1)
                            for a, src in ((Q, q_parts), (K, k_part.broadcast_to([HD, PARTS, 2 * S]))):
                                sp.dma_start(stage[rows, u, j, a, :, :].rearrange("p v n -> p (v n)"),
                                             src).then_inc(stage_in[u], 16)

                def store_group(b, hg):
                    wait(sp, pv_copied, b * G + hg + 2)
                    for j in range(HG):
                        h = hg * HG + j
                        sp.dma_start(o_raw[HD * h:HD * h + HD, :], pv_out[32 * j:32 * j + HD, :]).then_inc(out_moved, 16)
                        sp.dma_start(den[HD * h:HD * h + HD, :],
                                     pv_out[32 * j + HD:32 * j + HD + 1, :].rearrange("p (c t) -> p c t", c=HD)
                                     ).then_inc(out_moved, 16)

                def batch(b, last):
                    for hg in range(G):
                        if hg < 2:
                            stage_group(b, hg + 2, hg % 2)
                        elif not last:
                            if hg == 2:
                                wait(sp, parts_ready, 2 * b + 4)
                            stage_group(b + 1, hg - 2, hg % 2)
                        if hg == 0:
                            wait(sp, ot_ready, b + 1)
                        store_group(b, hg)
                    wait(sp, rec_ready, b + 1)
                    sp.dma_start(rec_dram.rearrange("h (c t) -> (h c) t", c=HD), rec[:, :]).then_inc(rec_stored, 16)
                    wait(sp, rec_stored, 16 * b + 16)
                    sp.dma_start(rec_b[:, :], rec_dram.rearrange("h (o n) -> h o n", o=1).broadcast_to([H, HD, S])
                                 ).then_inc(rec_in, 16)

                wait(sp, parts_ready, 2)
                wait(sp, pads_zero, 1)
                stage_group(0, 0, 0)
                stage_group(0, 1, 1)
                with sp.Fori(0, B - 1) as b:
                    batch(b, False)
                batch(B - 1, True)
            with sp.Else():
                wait(sp, q_sb, NC)
                wait(sp, k_sb, NC)
                sp.dma_start(qt_dram[:, :], qT[:, :]).then_inc(g_dram, 16)
                sp.dma_start(kt_dram[:, :], kT[:, :]).then_inc(g_dram, 16)
                sp.dma_start(g_table_s, decay_table[:, :]).then_inc(g_table, 16)
                wait(sp, g_dram, 32)
                with sp.Fori(0, B) as b:
                    with sp.Fori(0, H) as h:
                        wait(sp, g_norm, (b * H + h) * NB + 1)
                        sp.dma_start(g_q, qt_dram[bass.ds(h * HD, HD), bass.ds(b * S, S)]).then_inc(g_in, 16)
                        sp.dma_start(g_k, kt_dram[bass.ds(h * HD, HD), bass.ds(b * S, S)]).then_inc(g_in, 16)

            sp.wait_ge(ot_ready, B + 1)
            for b in range(B):
                sp.dma_start(X1[:, b * NB:(b + 1) * NB, :], x_t[:, b * NB:(b + 1) * NB, :]).then_inc(x2_in[b], 16)
            out_t = out.rearrange("(t p) d -> p t d", p=P)
            for b in range(B):
                sp.wait_ge(res_ready, b + 1)
                sp.dma_start(out_t[:, b * NB:(b + 1) * NB, :],
                             res[:, b, :].rearrange("p (t d) -> p t d", d=D)).then_inc(stored, 16)
            sp.wait_ge(stored, 16 * B)


        @block.gpsimd
        def _(pool):
            pool.wait_ge(w_in, 16 * 8)
            nc.gpsimd.tensor_tensor(wk_s[:, :], wk_s[:, :], wv_s[:, :], ALU.add).then_inc(wkv_ready, 1)
            pool.wait_ge(wkv_ready, 1)
            nc.gpsimd.memset(stage[2 * 32:KROWS, :, :, :, :, :].rearrange("p u j a v n -> p (u j a v n)").bitcast(F32),
                             0.0).then_inc(pads_zero, 1)
            pool.wait_ge(pads_zero, 1)
            for c in range(NC):
                for src, ready, off in ((qT, q_sb, 0), (kT, k_sb, B * S)):
                    pool.wait_ge(ready, c + 1)
                    cols = slice(c * CH, (c + 1) * CH)
                    nc.gpsimd.tensor_tensor(squares[:, off + c * CH:off + (c + 1) * CH], src[:, cols], src[:, cols],
                                            ALU.mult).then_inc(sq_ready, 1)

            pool.wait_ge(flag_ready, 1)
            bounded = pool.value_load(flag[0:1, 0:1], min_val=0, max_val=1)
            with pool.If(bounded > 0):
                def split(b, arrays, done, inc):
                    for i, (a, v) in enumerate(arrays):
                        src = (qT, kT)[a][:, bass.ds(b * S, S)]
                        row = decay[:, (a + v) % 2, :]
                        steps = [
                            (lambda: nc.gpsimd.tensor_tensor(split_s[:, :], src, row, ALU.mult)),
                            (lambda: nc.gpsimd.tensor_copy(parts[:, a, 0, v, :], split_s[:, :])),
                            (lambda: nc.gpsimd.tensor_tensor(split_s[:, :], split_s[:, :], parts[:, a, 0, v, :], ALU.subtract)),
                            (lambda: nc.gpsimd.tensor_copy(parts[:, a, 1, v, :], split_s[:, :])),
                            (lambda: nc.gpsimd.tensor_tensor(parts[:, a, 2, v, :], split_s[:, :], parts[:, a, 1, v, :], ALU.subtract)),
                        ]
                        for k, step in enumerate(steps):
                            ins = step()
                            ins.then_inc(pool_split, 1)
                            wait(pool, pool_split, done + 5 * i + k + 1)
                    pool.sem_inc(parts_ready, inc)

                def copy_values(b):
                    nc.gpsimd.tensor_copy(Vb[:, :, :, :].rearrange("p t h w -> p (t h w)"),
                                          V[:, bass.ds(b * NB, NB), :, :].rearrange("p t h w -> p (t h w)")
                                          ).then_inc(vb_ready, 1)

                def normalise(b):
                    wait(pool, out_moved, 16 * 2 * HG * G * (b + 1))
                    wait(pool, rec_in, 16 * b + 16)
                    nc.gpsimd.tensor_tensor(OT[:, bass.ds(b * S, S)], o_raw[:, :], rec_b[:, :],
                                            ALU.mult).then_inc(ot_ready, 1)

                wait(pool, v_sb, NC)
                copy_values(0)
                pool.wait_ge(c_in, 32)
                split(0, ((K, PLUS), (K, MINUS)), 0, 1)
                pool.sem_inc(ot_ready, 1)
                with pool.Fori(0, B - 1) as b:
                    wait(pool, stage_in[1], FILL * (2 * b + 2))
                    wait(pool, stage_in[0], FILL * (2 * b + 2))
                    split(b + 1, ((Q, PLUS), (Q, MINUS), (K, PLUS), (K, MINUS)), 10 + 20 * b, 2)
                    wait(pool, pv_done, NB * G * (b + 1) + 2)
                    copy_values(b + 1)
                    normalise(b)
                normalise(B - 1)

            for b in range(B):
                pool.wait_ge(magic_ready, b + 1)
                pool.wait_ge(scaled, b + 1)
                nc.gpsimd.tensor_tensor(rnd, xs, magic, ALU.add).then_inc(pool_tail, 1)
                pool.wait_ge(pool_tail, b + 1)
                nc.gpsimd.tensor_tensor(rnd, rnd, magic, ALU.subtract).then_inc(rounded, 1)

        @block.scalar
        def _(act):
            for dst, src in ((wk_s, wk), (wv_s, wv), (wd_s, wd), (wuk_s, wuk), (wuv_s, wuv), (eye, ident),
                             (wq_s, wq), (wo_s, wo)):
                act.dma_start(dst[:, :], src[:, :]).then_inc(w_in, 16)
            act.dma_start(hsum_f[:, :], head_sum[:, :]).then_inc(const_in, 16)
            act.dma_start(w8_s[:, :], w8[:, :]).then_inc(const_in, 16)
            act.dma_start(bias_s[:, :], bias.broadcast_to([P, D])).then_inc(const_in, 16)
            act.dma_start(scales[:, 0:1], s_in.broadcast_to([P, 1])).then_inc(const_in, 16)
            act.dma_start(scales[:, 1:2], s_k.broadcast_to([P, 1])).then_inc(const_in, 16)

            act.wait_ge(fold_pe, 1)
            nc.scalar.copy(wkv_T[:, :], ps[:, 6, 0:D]).then_inc(fold_act, 1)
            act.wait_ge(fold_pe, 2)
            nc.scalar.copy(wdown_T[:, :], ps[0:DL, 7, 0:D]).then_inc(fold_act, 1)
            act.wait_ge(fold_pe, 3)
            nc.scalar.copy(wk_eff[:, :], ps[:, 6, 0:D]).then_inc(fold_act, 1)
            nc.scalar.copy(wv_eff[:, :], ps[:, 6, D:2 * D]).then_inc(fold_act, 1)

            for n, (kind, c) in enumerate(JOBS):
                cols = slice(c * CH, (c + 1) * CH)
                if kind == "T":
                    act.wait_ge(tr_ready, c + 1)
                    nc.scalar.copy(xnT[:, cols], ps[:, n % 8, :]).then_inc(xnT_ready, 1)
                elif kind == "q":
                    act.wait_ge(q_ps, c + 1)
                    nc.scalar.copy(qT[:, cols], ps[:, n % 8, :]).then_inc(q_sb, 1)
                elif kind == "k":
                    act.wait_ge(k_ps, c + 1)
                    nc.scalar.copy(kT[:, cols], ps[:, n % 8, :]).then_inc(k_sb, 1)

            act.wait_ge(flag_ready, 1)
            bounded = act.value_load(flag[0:1, 0:1], min_val=0, max_val=1)
            with act.If(bounded > 0):
                act.sem_inc(exp_done, 2)
                with act.Fori(0, B) as b:
                    for hg in range(G):
                        for kc in range(NB):
                            tile = (b * G + hg) * NB + kc
                            act.wait_ge(pv_done, tile + 1)
                            for j in range(HG):
                                n = tile * HG + j
                                act.wait_ge(qk_done, n + 1)
                                act.wait_ge(diag_fixed, n + 1)
                                nc.scalar.activation(probs[:, (kc % 2) * HG + j, :], score[j % 2], ACT.Exp,
                                                     scale=SCALE).then_inc(exp_done, 1)
            with act.Else():
                with act.Fori(0, B * H) as i:
                    for t in range(NB):
                        n = i * NB + t
                        act.wait_ge(g_max, n + 1)
                        nc.scalar.activation(g_p, g_dec_s, ACT.Exp, bias=norms[:, 7:8]).then_inc(g_exp, 1)
                for c in range(NC):
                    act.wait_ge(g_otr, c + 1)
                    nc.scalar.copy(OT[:, c * CH:(c + 1) * CH], ps[:, c, :]).then_inc(g_ot, 1)
                act.wait_ge(g_ot, NC)
                act.sem_inc(ot_ready, B + 1)

            def finish_batch(act, b):
                act.wait_ge(xqT_ps, b + 1)
                if b:
                    act.wait_ge(y_ps, b)
                nc.scalar.copy(xqT, xqT_b).then_inc(xqT_ready, 1)
                act.wait_ge(y_ps, b + 1)
                if b:
                    act.wait_ge(res_ready, b)
                nc.scalar.mul(yb, yps, oscale[:, 0:1]).then_inc(y_ready, 1)

            for b in range(B):
                act.wait_ge(ln2_ready, b + 1)
                if b:
                    act.wait_ge(xq_ready, b)
                nc.scalar.mul(xs, xn2, rscales[:, 0:1]).then_inc(scaled, 1)
                if b:
                    finish_batch(act, b - 1)
            finish_batch(act, B - 1)

        @block.tensor
        def _(pe):
            pe.wait_ge(w_in, 16 * 8)
            pe.wait_ge(wkv_ready, 1)
            nc.tensor.transpose(ps[:, 6, 0:D], wk_s[:, :], eye[:, :]).then_inc(fold_pe, 1)
            pe.wait_ge(fold_act, 1)
            nc.tensor.matmul(ps[0:DL, 7, 0:D], wd_s[:, :], wkv_T[:, :], start=True, stop=True).then_inc(fold_pe, 1)
            pe.wait_ge(fold_act, 2)
            nc.tensor.matmul(ps[:, 6, 0:D], wdown_T[:, :], wuk_s[:, :], start=True, stop=True)
            nc.tensor.matmul(ps[:, 6, D:2 * D], wdown_T[:, :], wuv_s[:, :], start=True, stop=True).then_inc(fold_pe, 1)
            pe.wait_ge(fold_act, 4)

            evacuated = {"T": xnT_ready, "q": q_sb, "k": k_sb, "v": v_sb}
            for n, (kind, c) in enumerate(JOBS):
                cols = slice(c * CH, (c + 1) * CH)
                if n >= 8:
                    k0, c0 = JOBS[n - 8]
                    pe.wait_ge(evacuated[k0], c0 + 1)
                if kind == "T":
                    pe.wait_ge(xn_ready, c + 1)
                    for t in range(4):
                        last = nc.tensor.transpose(ps[:, n % 8, t * P:(t + 1) * P], X[:, 4 * c + t, :], eye[:, :])
                    last.then_inc(tr_ready, 1)
                elif kind == "q":
                    pe.wait_ge(xnT_ready, c + 1)
                    nc.tensor.matmul(ps[:, n % 8, :], wq_s[:, :], xnT[:, cols], start=True, stop=True).then_inc(q_ps, 1)
                elif kind == "k":
                    nc.tensor.matmul(ps[:, n % 8, :], wk_eff[:, :], xnT[:, cols], start=True, stop=True).then_inc(k_ps, 1)
                else:
                    for t in range(4):
                        last = nc.tensor.matmul(ps[:, n % 8, t * P:(t + 1) * P],
                                                xnT[:, c * CH + t * P:c * CH + (t + 1) * P], wv_eff[:, :],
                                                start=True, stop=True)
                    last.then_inc(v_ps, 1)

            pe.wait_ge(sq_ready, 2 * NC)
            pe.wait_ge(q_sb, NC)
            pe.wait_ge(k_sb, NC)
            pe.wait_ge(v_sb, NC)
            pe.wait_ge(const_ready, 1)
            for which in range(2):
                for half in range(2):
                    for b in range(B):
                        col = which * B * S + b * S + half * CH
                        last = nc.tensor.matmul(ps[32 * b:32 * b + 32, 2 * which + half, :], hsum[:, :],
                                                squares[:, col:col + CH], start=True, stop=True)
            last.then_inc(norm_ps, 1)
            pe.wait_ge(ok_ready, 1)
            nc.tensor.matmul(ps[0:1, 4, 0:1], norms[:, 6:7], ones[:, :], start=True, stop=True).then_inc(ok_ps, 1)

            pe.wait_ge(flag_ready, 1)
            bounded = pe.value_load(flag[0:1, 0:1], min_val=0, max_val=1)
            with pe.If(bounded > 0):
                def qk(u, j, kc, slot):
                    keys = slice(kc * P, (kc + 1) * P)
                    own, other = kc * P // CH * CH, (1 - kc * P // CH) * CH
                    pieces = [(own, kc * P, MINUS), (kc * P, own + CH, PLUS), (other, other + CH, PLUS if other else MINUS)]
                    for i, (lo, hi, v) in enumerate(pieces):
                        if lo == hi:
                            continue
                        ins = nc.tensor.matmul(slot[:, lo:hi], stage[0:KROWS, u, j, K, v, keys],
                                               stage[0:KROWS, u, j, Q, v, lo:hi], start=True, stop=True)
                        if i:
                            ins.then_inc((edge_ready, qk_done)[i - 1], 1)

                def weigh(b, hg, kc, half):
                    if half == 0:
                        tile = (b * G + hg) * NB + kc
                        pe.wait_ge(exp_done, (tile + 1) * HG + 2)
                        if kc == 0:
                            pe.wait_ge(pv_copied, b * G + hg + 1)
                            if hg == 0:
                                pe.wait_ge(vb_ready, b + 1)
                    for j in range(HG):
                        last = nc.tensor.matmul(pv[32 * j:32 * j + VW, half * CH:(half + 1) * CH],
                                                Vb[:, kc, hg * HG + j, :],
                                                probs[:, (kc % 2) * HG + j, half * CH:(half + 1) * CH],
                                                start=kc == 0, stop=kc == NB - 1)
                    if half == 1:
                        last.then_inc(pv_done, 1)

                pe.sem_inc(pv_done, 2)
                pe.wait_ge(pv_clear, 1)
                with pe.Fori(0, B) as b:
                    for hg in range(G):
                        u = hg % 2
                        pe.wait_ge(stage_in[u], FILL * (2 * b + hg // 2 + 1))
                        for kc in range(NB):
                            tile = (b * G + hg) * NB + kc
                            for j in range(HG):
                                pe.wait_ge(exp_done, tile * HG + j + 1)
                                qk(u, j, kc, score[j % 2])
                                if j % 2 == 1:
                                    if kc > 0:
                                        weigh(b, hg, kc - 1, j // 2)
                                    elif hg > 0:
                                        weigh(b, hg - 1, NB - 1, j // 2)
                    weigh(b, G - 1, NB - 1, 0)
                    weigh(b, G - 1, NB - 1, 1)
            with pe.Else():
                with pe.Fori(0, B) as b:
                    with pe.Fori(0, H) as h:
                        i = b * H + h
                        pe.wait_ge(g_in, 32 * (i + 1))
                        for t in range(NB):
                            n = i * NB + t
                            pe.wait_ge(g_scores_free, n + 1)
                            for half in range(2):
                                last = nc.tensor.matmul(ps[:, half, :], g_q[:, t * P:(t + 1) * P],
                                                        g_k[:, half * CH:(half + 1) * CH], start=True, stop=True)
                            last.then_inc(g_scores, 1)
                            pe.wait_ge(g_exp, n + 1)
                            for k in range(NB):
                                last = nc.tensor.transpose(ps_all[:, 2 * CH + k * P:2 * CH + (k + 1) * P],
                                                           g_p[:, k * P:(k + 1) * P], eye[:, :])
                            last.then_inc(g_tr, 1)
                            pe.wait_ge(g_pT, n + 1)
                            for k in range(NB):
                                last = nc.tensor.matmul(ps[:, 4, 0:VW], g_pT_s[:, k * P:(k + 1) * P],
                                                        V[:, bass.ds(b * NB + k, 1), bass.ds(h, 1), :],
                                                        start=k == 0, stop=k == NB - 1)
                            last.then_inc(g_o, 1)
                pe.wait_ge(g_norm, B * H * NB + 1)
                for c in range(NC):
                    for t in range(4):
                        k = 4 * c + t
                        last = nc.tensor.transpose(ps[:, c, t * P:(t + 1) * P], g_otok[:, k * D:(k + 1) * D], eye[:, :])
                    last.then_inc(g_otr, 1)

            pe.wait_ge(ot_ready, B + 1)
            pe.wait_ge(kq_ready, 1)

            def project(b):
                if b >= 2:
                    pe.wait_ge(x1_ready, b - 1)
                for t in range(NB):
                    k = b * NB + t
                    last = nc.tensor.matmul(proj[b % 2][:, t * P:(t + 1) * P], OT[:, k * P:(k + 1) * P], wo_s[:, :],
                                            start=True, stop=True)
                last.then_inc(proj_ps, 1)

            project(0)
            for b in range(B):
                if b + 1 < B:
                    project(b + 1)
                pe.wait_ge(xq_ready, b + 1)
                if b:
                    pe.wait_ge(xqT_ready, b)
                for t in range(NB):
                    last = nc.tensor.transpose(xqT_b[:, t * P:(t + 1) * P], xq[:, t * P:(t + 1) * P], eye16[:, :])
                last.then_inc(xqT_ps, 1)
                pe.wait_ge(xqT_ready, b + 1)
                if b:
                    pe.wait_ge(y_ready, b)
                for t in range(NB):
                    last = nc.tensor.matmul(yps[:, t * P:(t + 1) * P], xqT[:, t * P:(t + 1) * P], kq[:, :],
                                            start=True, stop=True)
                last.then_inc(y_ps, 1)

        @block.vector
        def _(dve):
            count = [0]

            def chain(ins):
                count[0] += 1
                ins.then_inc(dve_step, 1)
                dve.wait_ge(dve_step, count[0])

            def inverse_std(lo, n):
                var, y, y2 = rs[:, 0, lo:lo + n], rs[:, 1, lo:lo + n], rs[:, 2, lo:lo + n]
                chain(nc.vector.tensor_scalar(var, mv[:, lo:lo + n, 1], EPS, None, ALU.add))
                chain(nc.vector.tensor_scalar(y2.bitcast(I32), var.bitcast(I32), 1, None, ALU.logical_shift_right))
                chain(nc.vector.tensor_scalar(y.bitcast(I32), y2.bitcast(I32), -1.0, RSQRT_MAGIC, ALU.mult, ALU.add))
                for _ in range(3):
                    chain(nc.vector.tensor_tensor(y2, y, y, ALU.mult))
                    chain(nc.vector.scalar_tensor_tensor(out=y2, in0=y2, scalar=-0.5, in1=var, op0=ALU.mult, op1=ALU.mult))
                    chain(nc.vector.scalar_tensor_tensor(out=y, in0=y2, scalar=1.5, in1=y, op0=ALU.add, op1=ALU.mult))

            def token_stats(src, lo, n):
                for t in range(lo, lo + n):
                    last = nc.vector.bn_stats(stats[:, t, :], src[:, t, :])
                chain(last)
                for t in range(lo, lo + n):
                    last = nc.vector.bn_aggr(mv[:, t, :], stats[:, t, :])
                chain(last)
                inverse_std(lo, n)

            def to_fp8_grid(src, m):
                chain(nc.vector.tensor_scalar(m.bitcast(I32), src.bitcast(I32), 0x7F800000, None, ALU.bitwise_and))
                return nc.vector.tensor_scalar(m, m, 2.0 ** -6, 1.5 * 2.0 ** 20, ALU.max, ALU.mult)

            def overflow_to_nan(dst, r, tmp):
                chain(nc.vector.scalar_tensor_tensor(out=tmp, in0=r, scalar=NAN_SCALE, in1=r, op0=ALU.mult, op1=ALU.mult))
                return nc.vector.scalar_tensor_tensor(out=dst, in0=tmp, scalar=0.0, in1=r, op0=ALU.mult, op1=ALU.add)

            nc.vector.memset(V[:, :, :, HD:VW], 1.0)
            nc.vector.memset(ones[:, :], 1.0)
            for g in range(2):
                lo, n = g * NT // 2, NT // 2
                for b in (2 * g, 2 * g + 1):
                    dve.wait_ge(x_in[b], 16)
                token_stats(X, lo, n)
                for t in range(lo, lo + n):
                    last = nc.vector.tensor_scalar(X[:, t, :], X[:, t, :], mv[:, t, 0:1], rs[:, 1, t:t + 1],
                                                   ALU.subtract, ALU.mult)
                    if t % 4 == 3:
                        last.then_inc(xn_ready, 1)
                if g == 0:
                    dve.wait_ge(const_in, 16 * 5)
                    nc.vector.tensor_copy(hsum[:, :], hsum_f[:, :]).then_inc(const_ready, 1)
            for n, (kind, c) in enumerate(JOBS):
                if kind == "v":
                    dve.wait_ge(v_ps, c + 1)
                    nc.vector.tensor_copy(V[:, 4 * c:4 * c + 4, :, 0:HD],
                                          ps[:, n % 8, :].rearrange("p (t h d) -> p t h d", t=4, h=H)).then_inc(v_sb, 1)
            chain(nc.vector.reciprocal(rscales[:, :], scales[:, :]))
            chain(nc.vector.tensor_scalar(w8f, w8_s[:, :], rscales[:, 1:2], None, ALU.mult))
            chain(to_fp8_grid(w8f, w8m))
            chain(nc.vector.tensor_tensor(w8f, w8f, w8m, ALU.add))
            chain(nc.vector.tensor_tensor(w8f, w8f, w8m, ALU.subtract))
            nc.vector.tensor_copy(eye16[:, :], eye[:, :])
            nc.vector.tensor_tensor(oscale[:, :], scales[:, 0:1], scales[:, 1:2], ALU.mult)
            overflow_to_nan(kq[:, :], w8f, w8m).then_inc(kq_ready, 1)

            dve.wait_ge(norm_ps, 1)
            for i in range(2):
                nc.vector.tensor_reduce(norms[:, i:i + 1], ps_all[:, i * S:(i + 1) * S], AX.X, ALU.max)
                nc.vector.tensor_reduce(norms[:, 2 + i:3 + i], ps_all[:, i * S:(i + 1) * S], AX.X, ALU.add)
            chain(nc.vector.tensor_reduce(norms[:, 5:6], wv_eff[:, :], AX.X, ALU.max, apply_absolute_value=True))
            nc.vector.tensor_scalar(norms[:, 0:1], norms[:, 0:1], norms[:, 1:2], NORM_LIMIT, ALU.mult, ALU.is_le)
            nc.vector.tensor_scalar(norms[:, 2:3], norms[:, 2:3], norms[:, 3:4], 3.0e38, ALU.add, ALU.is_le)
            chain(nc.vector.tensor_scalar(norms[:, 5:6], norms[:, 5:6], VALUE_BOUND / (D * 12.0), None, ALU.is_le))
            chain(nc.vector.tensor_tensor(norms[:, 0:1], norms[:, 0:1], norms[:, 2:3], ALU.mult))
            nc.vector.tensor_tensor(norms[:, 6:7], norms[:, 0:1], norms[:, 5:6], ALU.mult).then_inc(ok_ready, 1)
            dve.wait_ge(ok_ps, 1)
            nc.vector.tensor_scalar(flag[0:1, 0:1], ps[0:1, 4, 0:1], P - 0.5, None, ALU.is_ge).then_inc(flag_ready, 1)

            dve.wait_ge(flag_ready, 1)
            bounded = dve.value_load(flag[0:1, 0:1], min_val=0, max_val=1)
            with dve.If(bounded > 0):
                nc.vector.memset(pv, 0.0).then_inc(pv_clear, 1)
                dve.wait_ge(c_in, 32)
                steps = 0
                for a, v in ((Q, PLUS), (Q, MINUS)):
                    row = decay[:, (a + v) % 2, :]
                    s0 = rec_b
                    for step in (lambda: nc.vector.tensor_tensor(s0[:, :], qT[:, 0:S], row, ALU.mult),
                                 lambda: nc.vector.tensor_copy(parts[:, a, 0, v, :], s0[:, :]),
                                 lambda: nc.vector.tensor_tensor(s0[:, :], s0[:, :], parts[:, a, 0, v, :], ALU.subtract),
                                 lambda: nc.vector.tensor_copy(parts[:, a, 1, v, :], s0[:, :]),
                                 lambda: nc.vector.tensor_tensor(parts[:, a, 2, v, :], s0[:, :], parts[:, a, 1, v, :], ALU.subtract)):
                        steps += 1
                        step().then_inc(split_step, 1)
                        dve.wait_ge(split_step, steps)
                dve.sem_inc(parts_ready, 1)
                dve.sem_inc(pv_copied, 1)

                def copy_pv(group, half, first):
                    if half == 0:
                        dve.wait_ge(pv_done, NB * (group + 1) + 2)
                        if not first:
                            dve.wait_ge(out_moved, 16 * 2 * HG * group)
                    ins = nc.vector.tensor_copy(pv_out[0:96 + VW, half * CH:(half + 1) * CH],
                                                pv[0:96 + VW, half * CH:(half + 1) * CH])
                    if half == 1:
                        ins.then_inc(pv_copied, 1)

                def invert_sums(b):
                    dve.wait_ge(out_moved, 16 * 2 * HG * G * (b + 1))
                    dve.wait_ge(ot_ready, b + 1)
                    nc.vector.reciprocal(rec[:, :], den[:, :]).then_inc(rec_ready, 1)

                def batch(b, first):
                    for hg in range(G):
                        for kc in range(NB):
                            tile = (b * G + hg) * NB + kc
                            for j in range(HG):
                                dve.wait_ge(edge_ready, tile * HG + j + 1)
                                cols = slice(kc * P, (kc + 1) * P)
                                nc.vector.tensor_tensor(score[j % 2][:, cols], score[j % 2][:, cols],
                                                        fix[:, :], ALU.mult).then_inc(diag_fixed, 1)
                                if hg > 0 and kc == 1 and j < 2:
                                    copy_pv(b * G + hg - 1, j, first and hg == 1)
                            if hg == 0 and kc == 2 and not first:
                                invert_sums(b - 1)
                    copy_pv(b * G + G - 1, 0, False)
                    copy_pv(b * G + G - 1, 1, False)

                batch(0, True)
                with dve.Fori(1, B) as b:
                    batch(b, False)
                invert_sums(B - 1)
            with dve.Else():
                dve.sem_inc(g_scores_free, 1)
                dve.sem_inc(g_norm, 1)
                dve.wait_ge(g_table, 16)
                with dve.Fori(0, B) as b:
                    with dve.Fori(0, H) as h:
                        for t in range(NB):
                            n = (b * H + h) * NB + t
                            done = 4 * n
                            dve.wait_ge(g_scores, n + 1)
                            nc.vector.tensor_scalar(g_clip, ps_all[:, 0:S], SCALE, -CLAMP, ALU.mult, ALU.max).then_inc(g_step, 1)
                            dve.wait_ge(g_step, done + 1)
                            dve.sem_inc(g_scores_free, 1)
                            u0 = S - P - t * P
                            nc.vector.scalar_tensor_tensor(out=g_dec_s, in0=g_clip, scalar=CLAMP,
                                                           in1=g_table_s[:, u0:u0 + S], op0=ALU.min,
                                                           op1=ALU.mult).then_inc(g_step, 1)
                            dve.wait_ge(g_step, done + 2)
                            nc.vector.tensor_reduce(norms[:, 6:7], g_dec_s, AX.X, ALU.max).then_inc(g_step, 1)
                            dve.wait_ge(g_step, done + 3)
                            nc.vector.tensor_scalar(norms[:, 7:8], norms[:, 6:7], -1.0, None, ALU.mult).then_inc(g_max, 1)
                            dve.wait_ge(g_tr, n + 1)
                            nc.vector.tensor_copy(g_pT_s, ps_all[:, 2 * CH:2 * CH + S]).then_inc(g_pT, 1)
                            dve.wait_ge(g_o, n + 1)
                            nc.vector.reciprocal(norms[:, 5:6], ps[:, 4, HD:VW]).then_inc(g_step, 1)
                            dve.wait_ge(g_step, done + 4)
                            nc.vector.tensor_scalar(g_otok[:, bass.ds((b * NB + t) * D + h * HD, HD)], ps[:, 4, 0:HD],
                                                    norms[:, 5:6], None, ALU.mult).then_inc(g_norm, 1)

            def residual_norm(b):
                dve.wait_ge(x2_in[b], 16)
                dve.wait_ge(proj_ps, b + 1)
                x1 = X1[:, b * NB:(b + 1) * NB, :].rearrange("p t d -> p (t d)")
                ins = nc.vector.tensor_tensor(x1, proj[b % 2], x1, ALU.add)
                ins.then_inc(x1_ready, 1)
                dve.wait_ge(x1_ready, b + 1)
                token_stats(X1, b * NB, NB)
                if b:
                    dve.wait_ge(scaled, b)
                for t in range(NB):
                    k = b * NB + t
                    last = nc.vector.tensor_scalar(xn2[:, t * D:(t + 1) * D], X1[:, k, :], mv[:, k, 0:1],
                                                   rs[:, 1, k:k + 1], ALU.subtract, ALU.mult)
                last.then_inc(ln2_ready, 1)

            def grid(b):
                dve.wait_ge(scaled, b + 1)
                if b:
                    dve.wait_ge(rounded, b)
                to_fp8_grid(xs, magic).then_inc(magic_ready, 1)

            def quantised(b):
                dve.wait_ge(rounded, b + 1)
                if b:
                    dve.wait_ge(xqT_ps, b)
                overflow_to_nan(xq, rnd, magic).then_inc(xq_ready, 1)

            def result(b):
                dve.wait_ge(y_ready, b + 1)
                y3 = yb.rearrange("p (t d) -> p t d", d=D)
                chain(nc.vector.tensor_tensor(y3, y3, bias_s[:, :].rearrange("p (o d) -> p o d", o=1)
                                              .broadcast_to([P, NB, D]), ALU.add))
                nc.vector.tensor_tensor(res[:, b, :], X1[:, b * NB:(b + 1) * NB, :].rearrange("p t d -> p (t d)"), yb,
                                        ALU.add).then_inc(res_ready, 1)

            residual_norm(0)
            for b in range(B):
                grid(b)
                if b + 1 < B:
                    residual_norm(b + 1)
                quantised(b)
                if b:
                    result(b - 1)
            result(B - 1)


_INS = ['L0_attn_x', 'L0_attn_Wq', 'L0_attn_Wk', 'L0_attn_Wv', 'L0_attn_Wo', 'L0_attn_W_down_kv', 'L0_attn_W_up_k',
        'L0_attn_W_up_v', 'L0_ffn_kernel', 'L0_ffn_input_scale', 'L0_ffn_kernel_scale', 'L0_ffn_bias']


def constants():
    import numpy as np
    c = 0.01 * 0.01
    i = np.arange(S, dtype=np.float64)
    rows = np.concatenate([np.exp(-c * i), np.exp(c * i)])[None, :]
    p = np.arange(P)[:, None]
    table = np.exp(-c * np.abs(p - np.arange(TABLE)[None, :] + S - P))
    key, query = p, np.arange(P)[None, :]
    fix = np.exp(-2 * c * np.maximum(key - query, 0))
    head_sum = (np.arange(P)[:, None] // HD == np.arange(32)[None, :]).astype(np.float64)
    return {"decay_rows": rows, "decay_table": table, "diag_fix": fix, "ident": np.eye(P), "head_sum": head_sum}


def kernel(**inputs):
    import numpy as np
    import concourse.bacc as bacc
    from concourse.bass_utils import run_bass_kernel_spmd

    nc = bacc.Bacc("TRN2", target_bir_lowering=False, num_devices=1)
    arrays = {}
    for name in _INS:
        a = np.ascontiguousarray(inputs[name])
        if a.ndim == 3:
            a = a.reshape(B * S, D)
        if a.ndim == 1:
            a = a.reshape(1, -1)
        arrays[name] = a
    for name, a in constants().items():
        arrays[name] = np.ascontiguousarray(a.astype(np.float32))
    args = [nc.dram_tensor(n, a.shape, mybir.dt.from_np(a.dtype), kind="ExternalInput").ap() for n, a in arrays.items()]
    out = nc.dram_tensor("out", (B * S, D), F32, kind="ExternalOutput").ap()
    qt_dram = nc.dram_tensor("qt_dram", (P, B * S), F32, kind="Internal").ap()
    kt_dram = nc.dram_tensor("kt_dram", (P, B * S), F32, kind="Internal").ap()
    rec_dram = nc.dram_tensor("rec_dram", (H, S), F32, kind="Internal").ap()
    build(nc, *args, out, qt_dram, kt_dram, rec_dram)
    r = run_bass_kernel_spmd(nc, [arrays], core_ids=[0])
    return r.results[0]["out"].reshape(B, S, D)
```

```python
import concourse.bass as bass
from concourse import mybir
from contextlib import ExitStack

F32 = mybir.dt.float32
BF16 = mybir.dt.bfloat16
I32 = mybir.dt.int32
ALU = mybir.AluOpType
ACT = mybir.ActivationFunctionType
AX = mybir.AxisListType

B, S, D = 4, 1024, 128
H, HD = 16, 8
DL = 32
P = 128
NT = B * S // P
NB = S // P
HG = 4
G = H // HG
CH = 512
NC = B * S // CH
PARTS = 3
ROWS = HD * PARTS * PARTS
KROWS = 96
VB = NB * H * (HD + 1)
VW = HD + 1
FILL = 16 * 2 * PARTS * HG
SCALE = 1.0 / (float(D) ** 0.5 + 1e-8)
CLAMP = 10000.0
EPS = 1e-5
SCORE_BOUND = 40.0
VALUE_BOUND = 1e16
NORM_LIMIT = (SCORE_BOUND / SCALE) ** 2 / 1.02
Q, K = range(2)
PLUS, MINUS = range(2)
NAN_SCALE = 3.0e38 / (464.0 * 464.0)
TABLE = 2 * S - P
RSQRT_MAGIC = float(0x5F3759DF)

JOBS = [("T", 0)]
for _c in range(NC):
    JOBS += [("T", _c + 1)] * (_c + 1 < NC) + [("q", _c), ("k", _c), ("v", _c)]

CHUNKS = G * NB * HG
INSERTED = [(1, 2), (1, 4), (2, 30), (3, 6)]
ITEMS = []
for _hg in range(G):
    for _m in range(NB * HG):
        if (_hg, _m) in INSERTED:
            ITEMS.append(("tail", INSERTED.index((_hg, _m))))
        ITEMS.append(("scores", _hg * NB * HG + _m))
XQT_CHUNK, Y_CHUNK = [(_hg - 1) * NB * HG + _m for _hg, _m in INSERTED[2:]]
TAIL_STEPS = 24
assert len(ITEMS) % 3 == 0


def item(hg, m):
    return ITEMS.index(("scores", hg * NB * HG + m))


def slot(hg, m, inserted=False):
    return (item(hg, m) - inserted) % 3


def build(nc, x, wq, wk, wv, wo, wd, wuk, wuv, w8, s_in, s_k, bias, decay_rows, decay_table,
          const_cols, zeros, out, qt_dram, kt_dram, v_dram, rec_dram):
    with ExitStack() as ctx:
        def sb(name, shape, dt=F32):
            return ctx.enter_context(nc.sbuf_tensor(name, shape, dt))

        def sem(name):
            return ctx.enter_context(nc.semaphore(name))

        late1 = sb("late1", [P, 4 * S])
        late2 = sb("late2", [P, 4, S])
        OT = sb("OT", [P, S])
        Vb = sb("Vb", [P, NB, H, VW])
        qk_b = late2[:, 0:2, :]
        stage = sb("stage", [P, 2, HG, 2, 2, S], BF16)
        probs = sb("probs", [P, 2 * HG, S])
        parts = sb("parts", [P, 2, 2 * PARTS * 2 * S], BF16)
        pv_out = sb("pv_out", [P, S])
        o_raw = late2[:, 2, :]
        rec_b = late2[:, 3, :]
        den = sb("den", [P, S // HD])
        rec = sb("rec", [P, S // HD])
        decay = sb("decay", [P, 2, S])
        split_s = sb("split_s", [P, S])
        consts = sb("consts", [P, 2 * P + 32])
        eye, fix, hsum_f = consts[:, 0:P], consts[:, P:2 * P], consts[:, 2 * P:2 * P + 32]
        eye16 = sb("eye16", [P, P], BF16)
        hsum = sb("hsum", [P, 32], BF16)
        wq_s = sb("wq_s", [P, D])
        wo_s = sb("wo_s", [P, D])
        wk_eff = sb("wk_eff", [P, D])
        wv_eff = sb("wv_eff", [P, D])
        w8_s = sb("w8_s", [P, D], BF16)
        kq = sb("kq", [P, D], BF16)
        bias_s = sb("bias_s", [P, D], BF16)
        scales = sb("scales", [P, 2])
        rscales = sb("rscales", [P, 2])
        oscale = sb("oscale", [P, 1])
        stats = sb("stats", [P, NT, 6])
        mv = sb("mv", [P, NT, 2])
        rs = sb("rs", [P, 3, NT])
        norms = sb("norms", [P, 8])
        flag = sb("flag", [1, 1], I32)
        ones = sb("ones", [P, 1])

        X = probs[:, 0:HG, :].rearrange("p a (t d) -> p (a t) d", d=D)
        xnT = probs[:, HG:2 * HG, :].rearrange("p a n -> p (a n)")
        qT, kT = late1[:, :], late2[:, :, :].rearrange("p a n -> p (a n)")

        def squares(which, c):
            return xnT[:, c * CH:(c + 1) * CH].bitcast(BF16)[:, which * CH:(which + 1) * CH]

        V = parts[:, 1, :].bitcast(F32)[:, 0:NT * H * VW].rearrange("p (t h w) -> p t h w", t=NT, h=H)

        def part(buf, a, k, v=None):
            at = (a * PARTS + k) * 2 * S
            return parts[:, buf, at:at + 2 * S] if v is None else parts[:, buf, at + v * S:at + (v + 1) * S]

        wk_s, wv_s, wkv_T = [pv_out[:, i * D:(i + 1) * D] for i in range(3)]
        wuk_s, wuv_s, wdown_T = [pv_out[0:DL, i * D:(i + 1) * D] for i in range(3, 6)]
        wd_s = pv_out[:, 6 * D:6 * D + DL]
        w8f, w8m = [split_s[:, i * D:(i + 1) * D] for i in range(2)]
        gen = stage[:, :, :, :, :, :].rearrange("p u j a v n -> p (u j a v n)").bitcast(F32)
        g_clip, g_dec_s, g_p, g_pT_s = [gen[:, i * S:(i + 1) * S] for i in range(4)]
        g_otok = gen[:, 4 * S:5 * S]
        g_table_s = gen[:, 8 * S:8 * S + TABLE]
        g_q, g_k = gen[0:HD, 10 * S:11 * S], gen[0:HD, 11 * S:12 * S]

        ps = ctx.enter_context(nc.psum_tensor("ps", [P, 8, CH], F32))
        ps_all = ps[:, :, :].rearrange("p b n -> p (b n)")
        score = [ps_all[:, i * S:(i + 1) * S] for i in range(3)]
        pv = ps_all[:, 6 * CH:8 * CH]

        x_in = [sem(f"x_in{b}") for b in range(B)]
        w_in = sem("w_in")
        wq_in = sem("wq_in")
        c0_in = sem("c0_in")
        c_in = sem("c_in")
        waited = sem("waited")
        const_in = sem("const_in")
        fold_in = sem("fold_in")
        kq_ready = sem("kq_ready")
        pv_clear = sem("pv_clear")
        g_ot = sem("g_ot")
        dve_step = sem("dve_step")
        pool_split = sem("pool_split")
        pool_tail = sem("pool_tail")
        wkv_ready = sem("wkv_ready")
        fold_pe = sem("fold_pe")
        fold_act = sem("fold_act")
        xn_ready = sem("xn_ready")
        tr_ready = sem("tr_ready")
        xnT_ready = sem("xnT_ready")
        q_ps = sem("q_ps")
        k_ps = sem("k_ps")
        v_ps = sem("v_ps")
        q_sb = sem("q_sb")
        k_sb = sem("k_sb")
        v_sb = sem("v_sb")
        v_ones = sem("v_ones")
        q_parts = sem("q_parts")
        pv_first = sem("pv_first")
        sq_ready = sem("sq_ready")
        norm_ps = sem("norm_ps")
        ok_ready = sem("ok_ready")
        ok_ps = sem("ok_ps")
        flag_ready = sem("flag_ready")
        const_ready = sem("const_ready")
        parts_ready = sem("parts_ready")
        vb_in = [sem(f"vb_in{hg}") for hg in range(G)]
        qk_in = sem("qk_in")
        dram_out = sem("dram_out")
        pads_in = [sem(f"pads_in{u}") for u in range(2)]
        stage_in = [sem(f"stage_in{u}") for u in range(2)]
        edge_ready = sem("edge_ready")
        diag_fixed = sem("diag_fixed")
        qk_done = sem("qk_done")
        exp_done = sem("exp_done")
        pv_done = sem("pv_done")
        pv_copied = sem("pv_copied")
        out_moved = sem("out_moved")
        rec_ready = sem("rec_ready")
        rec_stored = sem("rec_stored")
        rec_in = sem("rec_in")
        ot_ready = sem("ot_ready")
        g_table = sem("g_table")
        g_in = sem("g_in")
        g_step = sem("g_step")
        g_init = sem("g_init")
        g_scores = sem("g_scores")
        g_scores_free = sem("g_scores_free")
        g_max = sem("g_max")
        g_exp = sem("g_exp")
        g_tr = sem("g_tr")
        g_pT = sem("g_pT")
        g_o = sem("g_o")
        g_norm = sem("g_norm")
        g_otr = sem("g_otr")
        x2_in = sem("x2_in")
        tail_step = sem("tail_step")
        proj_ps = sem("proj_ps")
        x1_ready = sem("x1_ready")
        ln2_ready = sem("ln2_ready")
        magic_ready = sem("magic_ready")
        rounded = sem("rounded")
        xq_ready = sem("xq_ready")
        xqT_ps = sem("xqT_ps")
        xqT_ready = sem("xqT_ready")
        y_ps = sem("y_ps")
        y_ready = sem("y_ready")
        res_ready = sem("res_ready")
        stored = sem("stored")

        block = ctx.enter_context(nc.Block())

        X1 = late1[:, 0:S]
        xs = late1[:, S:2 * S]
        magic = late1[:, 2 * S:3 * S]
        xn2 = late1[:, 3 * S:4 * S].bitcast(BF16)[:, 0:S]
        xq = xn2
        xqT = late1[:, 3 * S:4 * S].bitcast(BF16)[:, S:2 * S]
        yb = xqT
        halves = [slice(half * CH, (half + 1) * CH) for half in range(2)]

        def bank(n):
            return ps[:, n, :]

        def bank16(n):
            return ps[:, n, :].bitcast(BF16)[:, 0:CH]

        def wait(engine, semaphore, value):
            engine.wait_ge(semaphore, value)
            engine.sem_inc(waited, 1)

        @block.sync
        def _(sp):
            x_t = x.rearrange("(t p) d -> p t d", p=P)
            for b in range(B):
                sp.dma_start(X[:, b * NB:(b + 1) * NB, :], x_t[:, b * NB:(b + 1) * NB, :]).then_inc(x_in[b], 16)
                if b == 0:
                    sp.dma_start(wq_s[:, :], wq[:, :]).then_inc(wq_in, 16)
                    sp.dma_start(decay[:, :, :].rearrange("p a n -> p (a n)"),
                                 decay_rows.broadcast_to([P, 2 * S])).then_inc(c_in, 16)

            def clear_pads(u):
                n = KROWS - ROWS
                sp.dma_start(stage[ROWS:KROWS, u, :, :, :, :].rearrange("p j a v n -> p (j a v n)").bitcast(F32),
                             zeros.broadcast_to([n, HG * 2 * S])).then_inc(pads_in[u], 16)

            def stage_group(b, hg, u, buf, which=(Q, K), js=range(HG)):
                if js[0] == 0 and not (isinstance(b, int) and b == 0 and hg < 2):
                    wait(sp, qk_done, HG * NB * (b * G + hg - 1))
                for j in js:
                    h = hg * HG + j
                    heads = slice(HD * h, HD * h + HD)
                    for k in range(PARTS):
                        rows = slice(k, ROWS, PARTS)
                        all_q = parts[heads, buf, 0:PARTS * 2 * S].rearrange("p (k n) -> p k n", k=PARTS)
                        at = (PARTS + k) * 2 * S
                        k_part = parts[heads, buf, at:at + 2 * S].rearrange("p (o n) -> p o n", o=1)
                        for a in which:
                            src = (all_q, k_part.broadcast_to([HD, PARTS, 2 * S]))[a]
                            sp.dma_start(stage[rows, u, j, a, :, :].rearrange("p v n -> p (v n)"),
                                         src).then_inc(stage_in[u], 16)

            clear_pads(0)
            clear_pads(1)
            sp.wait_ge(v_ones, 1)
            for b in range(B):
                cols = slice(b * S, (b + 1) * S)
                sp.wait_ge(q_sb, 2 * b + 2)
                sp.dma_start(qt_dram[:, cols], qT[:, cols]).then_inc(dram_out, 16)
                sp.wait_ge(k_sb, 2 * b + 2)
                sp.dma_start(kt_dram[:, cols], kT[:, cols]).then_inc(dram_out, 16)
                sp.wait_ge(v_sb, 2 * b + 2)
                v_b = V[:, b * NB:(b + 1) * NB, :, :]
                sp.dma_start(v_dram[:, b * VB:(b + 1) * VB], v_b.rearrange("p t h w -> p (t h w)")).then_inc(dram_out, 16)
                if b == 0:
                    for hg in range(G):
                        heads = slice(hg * HG, (hg + 1) * HG)
                        sp.dma_start(Vb[:, :, heads, :].rearrange("p t h w -> p t (h w)"),
                                     v_b[:, :, heads, :].rearrange("p t h w -> p t (h w)")).then_inc(vb_in[hg], 16)
                if b == 2:
                    sp.wait_ge(q_parts, 1)
                    stage_group(0, 0, 0, 0, (Q,))
                    sp.wait_ge(parts_ready, 2)
                    stage_group(0, 0, 0, 0, (K,))
            stage_group(0, 1, 1, 0)
            sp.wait_ge(dram_out, 16 * 3 * B)

            def load_x(b):
                sp.dma_start(X1.rearrange("p (t d) -> p t d", d=D),
                             x[bass.ds(b * S, S), :].rearrange("(t p) d -> p t d", p=P)).then_inc(x2_in, 16)

            def store_result(b):
                wait(sp, res_ready, 2 * b + 2)
                sp.dma_start(out[bass.ds(b * S, S), :].rearrange("(t p) d -> p t d", p=P),
                             X1.rearrange("p (t d) -> p t d", d=D)).then_inc(stored, 16)
                wait(sp, stored, 16 * b + 16)

            sp.wait_ge(flag_ready, 1)
            bounded = sp.value_load(flag[0:1, 0:1], min_val=0, max_val=1)
            with sp.If(bounded > 0):
                def load_values(b, hg):
                    heads = slice(hg * HG, (hg + 1) * HG)
                    sp.dma_start(Vb[:, :, heads, :].rearrange("p t h w -> p t (h w)"),
                                 v_dram[:, bass.ds(b * VB, VB)].rearrange("p (t h w) -> p t h w", t=NB, h=H)
                                 [:, :, heads, :].rearrange("p t h w -> p t (h w)")).then_inc(vb_in[hg], 16)

                def load_qk(b):
                    for a, src in ((Q, qt_dram), (K, kt_dram)):
                        sp.dma_start(qk_b[:, a, :], src[:, bass.ds(b * S, S)]).then_inc(qk_in, 16)

                def store_group(b, hg):
                    wait(sp, pv_copied, 2 * (b * G + hg + 2))
                    for j in range(HG):
                        h = hg * HG + j
                        sp.dma_start(o_raw[HD * h:HD * h + HD, :], pv_out[32 * j:32 * j + HD, :]).then_inc(out_moved, 16)
                        sp.dma_start(den[HD * h:HD * h + HD, :],
                                     pv_out[32 * j + HD:32 * j + HD + 1, :].rearrange("p (c t) -> p c t", c=HD)
                                     ).then_inc(out_moved, 16)

                def batch(b, first, last):
                    for hg in range(G):
                        if hg == 0:
                            if not last:
                                load_qk(b + 1)
                        if hg == 2 and not last:
                            wait(sp, stage_in[0], FILL * (2 * b + 2))
                            wait(sp, stage_in[1], FILL * (2 * b + 2))
                            wait(sp, parts_ready, 2 * b + 4)
                        if hg == G - 1:
                            if not first:
                                store_result(b - 1)
                            load_x(b)
                        for js in ((0, 1), (2, 3)):
                            if hg < 2:
                                stage_group(b, hg + 2, hg % 2, b % 2, js=js)
                            elif not last:
                                stage_group(b + 1, hg - 2, hg % 2, (b + 1) % 2, js=js)
                            if js[0] == 0:
                                if hg == 0 and not first:
                                    wait(sp, ot_ready, b)
                                store_group(b, hg)
                        if not last:
                            load_values(b + 1, hg)

                batch(0, True, False)
                with sp.Fori(1, B - 1) as b:
                    batch(b, False, False)
                batch(B - 1, False, True)
            with sp.Else():
                wait(sp, stage_in[0], FILL)
                wait(sp, stage_in[1], FILL)
                wait(sp, pads_in[0], 16)
                wait(sp, pads_in[1], 16)
                sp.dma_start(g_table_s, decay_table[:, :]).then_inc(g_table, 16)

                def heads(b):
                    with sp.Fori(0, H) as h:
                        wait(sp, g_norm, (b * H + h) * NB + 1)
                        sp.dma_start(g_q, qt_dram[bass.ds(h * HD, HD), bass.ds(b * S, S)]).then_inc(g_in, 16)
                        sp.dma_start(g_k, kt_dram[bass.ds(h * HD, HD), bass.ds(b * S, S)]).then_inc(g_in, 16)

                with sp.Fori(0, B - 1) as b:
                    heads(b)
                    load_x(b)
                    store_result(b)
                heads(B - 1)
                load_x(B - 1)

            store_result(B - 1)

        @block.gpsimd
        def _(pool):
            pool.wait_ge(w_in, 16 * 2)
            nc.gpsimd.tensor_tensor(wk_s, wk_s, wv_s, ALU.add).then_inc(wkv_ready, 1)

            def square(c):
                pool.wait_ge(q_sb, c + 1)
                pool.wait_ge(v_ps, c + 1)
                cols = slice(c * CH, (c + 1) * CH)
                nc.gpsimd.tensor_tensor(squares(Q, c), qT[:, cols], qT[:, cols], ALU.mult).then_inc(sq_ready, 1)

            def split(buf, src, a, v, scratch, done):
                row = decay[:, (a + v) % 2, :]
                out0, out1, out2 = [parts[:, buf, (a * PARTS + k) * 2 * S + v * S:(a * PARTS + k) * 2 * S + (v + 1) * S]
                                    for k in range(PARTS)]
                for i, (dst, x0, x1, op) in enumerate(((scratch, src, row, ALU.mult), (out0, src, row, ALU.mult),
                                                       (scratch, scratch, out0, ALU.subtract),
                                                       (out1, scratch, out0, None),
                                                       (out2, scratch, out1, ALU.subtract))):
                    ins = nc.gpsimd.tensor_copy(dst, x0) if op is None else nc.gpsimd.tensor_tensor(dst, x0, x1, op)
                    ins.then_inc(pool_split, 1)
                    wait(pool, pool_split, done + i + 1)

            square(0)
            square(1)
            pool.wait_ge(c_in, 16)
            pool.wait_ge(k_sb, 2)
            split(0, kT[:, 0:S], K, MINUS, pv_out[:, :], 0)
            pool.sem_inc(parts_ready, 1)
            for c in range(2, NC):
                square(c)

            def to_grid(b, half):
                cols = halves[half]
                wait(pool, magic_ready, 2 * b + half + 1)
                nc.gpsimd.tensor_tensor(xs[:, cols], xs[:, cols], magic[:, cols], ALU.add).then_inc(pool_tail, 1)
                wait(pool, pool_tail, 2 * b + half + 1)
                nc.gpsimd.tensor_tensor(xs[:, cols], xs[:, cols], magic[:, cols], ALU.subtract).then_inc(rounded, 1)

            pool.wait_ge(flag_ready, 1)
            bounded = pool.value_load(flag[0:1, 0:1], min_val=0, max_val=1)
            with pool.If(bounded > 0):
                def normalise(b):
                    wait(pool, rec_ready, 2 * b + 2)
                    pool.dma_start(rec_dram.rearrange("h (c t) -> (h c) t", c=HD), rec[:, :]).then_inc(rec_stored, 16)
                    wait(pool, rec_stored, 16 * b + 16)
                    pool.dma_start(rec_b, rec_dram.rearrange("h (o n) -> h o n", o=1).broadcast_to([H, HD, S])
                                   ).then_inc(rec_in, 16)
                    wait(pool, out_moved, 16 * 2 * HG * G * (b + 1))
                    wait(pool, rec_in, 16 * b + 16)
                    nc.gpsimd.tensor_tensor(OT[:, :], o_raw, rec_b, ALU.mult).then_inc(ot_ready, 1)

                def split_next(b, buf, i):
                    a, v = ((Q, PLUS), (Q, MINUS), (K, PLUS), (K, MINUS))[i]
                    split(buf, qk_b[:, a, :], a, v, split_s[:, :], 5 + 20 * b + 5 * i)

                wait(pool, kq_ready, 1)
                wait(pool, qk_in, 32)
                for i in range(4):
                    split_next(0, 1, i)
                pool.sem_inc(parts_ready, 2)
                with pool.Fori(1, B - 1) as b:
                    normalise(b - 1)
                    wait(pool, qk_in, 32 * (b + 1))
                    for i in range(3):
                        split_next(b, (b + 1) % 2, i)
                    to_grid(b - 1, 0)
                    to_grid(b - 1, 1)
                    split_next(b, (b + 1) % 2, 3)
                    pool.sem_inc(parts_ready, 2)
                normalise(B - 2)
                to_grid(B - 2, 0)
                to_grid(B - 2, 1)
                normalise(B - 1)
            with pool.Else():
                with pool.Fori(0, B - 1) as b:
                    to_grid(b, 0)
                    to_grid(b, 1)

            to_grid(B - 1, 0)
            to_grid(B - 1, 1)

        @block.scalar
        def _(act):
            act.dma_start(wk_s, wk[:, :]).then_inc(w_in, 16)
            act.dma_start(wv_s, wv[:, :]).then_inc(w_in, 16)
            act.dma_start(consts[:, :], const_cols[:, :]).then_inc(c0_in, 16)
            for dst, src in ((wd_s, wd), (wuk_s, wuk), (wuv_s, wuv)):
                act.dma_start(dst, src[:, :]).then_inc(fold_in, 16)
            act.dma_start(wo_s[:, :], wo[:, :]).then_inc(const_in, 16)
            act.dma_start(w8_s[:, :], w8[:, :]).then_inc(const_in, 16)
            act.dma_start(bias_s[:, :], bias.broadcast_to([P, D])).then_inc(const_in, 16)
            act.dma_start(scales[:, 0:1], s_in.broadcast_to([P, 1])).then_inc(const_in, 16)
            act.dma_start(scales[:, 1:2], s_k.broadcast_to([P, 1])).then_inc(const_in, 16)

            act.wait_ge(fold_pe, 1)
            nc.scalar.copy(wkv_T, ps[:, 6, 0:D]).then_inc(fold_act, 1)
            act.wait_ge(fold_pe, 2)
            nc.scalar.copy(wdown_T, ps[0:DL, 7, 0:D]).then_inc(fold_act, 1)
            act.wait_ge(fold_pe, 3)
            nc.scalar.copy(wk_eff[:, :], ps[:, 6, 0:D]).then_inc(fold_act, 1)
            nc.scalar.copy(wv_eff[:, :], ps[:, 6, D:2 * D]).then_inc(fold_act, 1)

            for n, (kind, c) in enumerate(JOBS):
                cols = slice(c * CH, (c + 1) * CH)
                if kind == "T":
                    act.wait_ge(tr_ready, c + 1)
                    nc.scalar.copy(xnT[:, cols], ps[:, n % 8, :]).then_inc(xnT_ready, 1)
                elif kind == "q":
                    act.wait_ge(q_ps, c + 1)
                    nc.scalar.copy(qT[:, cols], ps[:, n % 8, :]).then_inc(q_sb, 1)
                elif kind == "k":
                    act.wait_ge(k_ps, c + 1)
                    nc.scalar.copy(kT[:, cols], ps[:, n % 8, :]).then_inc(k_sb, 1)
                else:
                    act.wait_ge(v_ps, c + 1)
                    act.wait_ge(k_sb, c + 1)
                    nc.scalar.square(squares(K, c), kT[:, cols])
                    nc.scalar.copy(V[:, 4 * c:4 * c + 4, :, 0:HD],
                                   ps[:, n % 8, :].rearrange("p (t h d) -> p t h d", t=4, h=H)).then_inc(v_sb, 1)

            def finish_batch(b):
                for half in range(2):
                    act.wait_ge(xqT_ps, 2 * b + half + 1)
                    nc.scalar.copy(xqT[:, halves[half]], bank16(4 + half)).then_inc(xqT_ready, 1)
                for half in range(2):
                    act.wait_ge(y_ps, 2 * b + half + 1)
                    nc.scalar.mul(yb[:, halves[half]], bank(6 + half), oscale[:, 0:1]).then_inc(y_ready, 1)

            act.wait_ge(flag_ready, 1)
            bounded = act.value_load(flag[0:1, 0:1], min_val=0, max_val=1)
            with act.If(bounded > 0):
                with act.Fori(0, B) as b:
                    for hg in range(G):
                        for m in range(NB * HG):
                            kc, j = m // HG, m % HG
                            n = (b * G + hg) * NB * HG + m
                            if j == 0:
                                act.wait_ge(pv_done, (b * G + hg) * NB + kc + 1)
                            act.wait_ge(qk_done, n + 1)
                            act.wait_ge(diag_fixed, n + 1)
                            nc.scalar.activation(probs[:, m % (2 * HG), :], score[slot(hg, m)], ACT.Exp,
                                                 scale=SCALE).then_inc(exp_done, 1)
            with act.Else():
                def heads(b):
                    with act.Fori(0, H) as h:
                        for t in range(NB):
                            act.wait_ge(g_max, (b * H + h) * NB + t + 1)
                            nc.scalar.activation(g_p, g_dec_s, ACT.Exp, bias=norms[:, 7:8]).then_inc(g_exp, 1)
                    for half in range(2):
                        act.wait_ge(g_otr, 2 * b + half + 1)
                        nc.scalar.copy(OT[:, halves[half]], bank(half)).then_inc(g_ot, 1)
                    act.wait_ge(g_ot, 2 * b + 2)
                    act.sem_inc(ot_ready, 1)

                with act.Fori(0, B - 1) as b:
                    heads(b)
                    finish_batch(b)
                heads(B - 1)

            finish_batch(B - 1)

        @block.tensor
        def _(pe):
            pe.wait_ge(wkv_ready, 1)
            pe.wait_ge(c0_in, 16)
            nc.tensor.transpose(ps[:, 6, 0:D], wk_s, eye).then_inc(fold_pe, 1)
            pe.wait_ge(fold_act, 1)
            pe.wait_ge(fold_in, 48)
            nc.tensor.matmul(ps[0:DL, 7, 0:D], wd_s, wkv_T, start=True, stop=True).then_inc(fold_pe, 1)
            pe.wait_ge(fold_act, 2)
            nc.tensor.matmul(ps[:, 6, 0:D], wdown_T, wuk_s, start=True, stop=True)
            nc.tensor.matmul(ps[:, 6, D:2 * D], wdown_T, wuv_s, start=True, stop=True).then_inc(fold_pe, 1)
            pe.wait_ge(fold_act, 4)
            pe.wait_ge(wq_in, 16)

            evacuated = {"T": xnT_ready, "q": q_sb, "k": k_sb, "v": v_sb}
            for n, (kind, c) in enumerate(JOBS):
                cols = slice(c * CH, (c + 1) * CH)
                if n >= 8:
                    k0, c0 = JOBS[n - 8]
                    pe.wait_ge(evacuated[k0], c0 + 1)
                if kind == "T":
                    pe.wait_ge(xn_ready, c + 1)
                    for t in range(4):
                        last = nc.tensor.transpose(ps[:, n % 8, t * P:(t + 1) * P], X[:, 4 * c + t, :], eye)
                    last.then_inc(tr_ready, 1)
                elif kind == "q":
                    pe.wait_ge(xnT_ready, c + 1)
                    nc.tensor.matmul(ps[:, n % 8, :], wq_s[:, :], xnT[:, cols], start=True, stop=True).then_inc(q_ps, 1)
                elif kind == "k":
                    nc.tensor.matmul(ps[:, n % 8, :], wk_eff[:, :], xnT[:, cols], start=True, stop=True).then_inc(k_ps, 1)
                else:
                    for t in range(4):
                        last = nc.tensor.matmul(ps[:, n % 8, t * P:(t + 1) * P],
                                                xnT[:, c * CH + t * P:c * CH + (t + 1) * P], wv_eff[:, :],
                                                start=True, stop=True)
                    last.then_inc(v_ps, 1)

            pe.wait_ge(sq_ready, NC)
            pe.wait_ge(q_sb, NC)
            pe.wait_ge(k_sb, NC)
            pe.wait_ge(v_sb, NC)
            pe.wait_ge(const_ready, 1)
            for which in range(2):
                for half in range(2):
                    for b in range(B):
                        last = nc.tensor.matmul(ps[32 * b:32 * b + 32, 2 * which + half, :], hsum[:, :],
                                                squares(which, 2 * b + half), start=True, stop=True)
            last.then_inc(norm_ps, 1)
            pe.wait_ge(ok_ready, 1)
            nc.tensor.matmul(ps[0:1, 4, 0:1], norms[:, 6:7], ones[:, :], start=True, stop=True).then_inc(ok_ps, 1)

            def project(b, half, bank_no):
                if half == 0:
                    pe.wait_ge(ot_ready, b + 1)
                for t in range(4):
                    k = 4 * half + t
                    last = nc.tensor.matmul(ps[:, bank_no, t * P:(t + 1) * P], OT[:, k * P:(k + 1) * P], wo_s[:, :],
                                            start=True, stop=True)
                last.then_inc(proj_ps, 1)

            def transpose_xq(b, *banks):
                for half in range(2):
                    pe.wait_ge(xq_ready, 2 * b + half + 1)
                    for t in range(4):
                        k = 4 * half + t
                        last = nc.tensor.transpose(bank16(banks[half])[:, t * P:(t + 1) * P], xq[:, k * P:(k + 1) * P],
                                                   eye16[:, :])
                    last.then_inc(xqT_ps, 1)

            def multiply(b, *banks):
                for half in range(2):
                    pe.wait_ge(xqT_ready, 2 * b + half + 1)
                    for t in range(4):
                        k = 4 * half + t
                        last = nc.tensor.matmul(ps[:, banks[half], t * P:(t + 1) * P], xqT[:, k * P:(k + 1) * P],
                                                kq[:, :], start=True, stop=True)
                    last.then_inc(y_ps, 1)

            def tail(b):
                project(b, 0, 2)
                project(b, 1, 3)
                transpose_xq(b, 4, 5)
                multiply(b, 6, 7)

            pe.wait_ge(kq_ready, 1)
            pe.wait_ge(const_in, 16 * 5)
            pe.wait_ge(flag_ready, 1)
            bounded = pe.value_load(flag[0:1, 0:1], min_val=0, max_val=1)
            with pe.If(bounded > 0):
                def qk(u, j, kc, slot):
                    keys = slice(kc * P, (kc + 1) * P)
                    own, other = kc * P // CH * CH, (1 - kc * P // CH) * CH
                    pieces = [(own, kc * P, MINUS), (kc * P, own + CH, PLUS), (other, other + CH, PLUS if other else MINUS)]
                    for i, (lo, hi, v) in enumerate(pieces):
                        if lo == hi:
                            continue
                        ins = nc.tensor.matmul(slot[:, lo:hi], stage[0:KROWS, u, j, K, v, keys],
                                               stage[0:KROWS, u, j, Q, v, lo:hi], start=True, stop=True)
                        if i:
                            ins.then_inc((edge_ready, qk_done)[i - 1], 1)

                def weigh(b, hg, kc, half):
                    if half == 0:
                        tile = (b * G + hg) * NB + kc
                        pe.wait_ge(exp_done, (tile + 1) * HG)
                        if kc == 0:
                            pe.wait_ge(vb_in[hg], 16 * b + 16)
                    if kc == 0:
                        pe.wait_ge(pv_copied, 2 * (b * G + hg) + half + 1)
                    for j in range(HG):
                        last = nc.tensor.matmul(pv[32 * j:32 * j + VW, half * CH:(half + 1) * CH],
                                                Vb[:, kc, hg * HG + j, :],
                                                probs[:, (kc % 2) * HG + j, half * CH:(half + 1) * CH],
                                                start=kc == 0, stop=kc == NB - 1)
                    last.then_inc((pv_first, pv_done)[half], 1)

                def batch(b, first):
                    for hg in range(G):
                        u = hg % 2
                        pe.wait_ge(stage_in[u], FILL * (2 * b + hg // 2 + 1))
                        for m in range(NB * HG):
                            kc, j = m // HG, m % HG
                            n = (b * G + hg) * NB * HG + m
                            if (hg, m) in INSERTED and not first:
                                tail_item(b - 1, INSERTED.index((hg, m)), slot(hg, m, True), b)
                            free_slot(b, first, item(hg, m))
                            qk(u, j, kc, score[slot(hg, m)])
                            if j % 2 == 1:
                                if kc > 0:
                                    weigh(b, hg, kc - 1, j // 2)
                                elif hg > 0:
                                    weigh(b, hg - 1, NB - 1, j // 2)
                                elif not first:
                                    weigh(b - 1, G - 1, NB - 1, j // 2)

                def free_slot(b, first, i):
                    if i < 3:
                        if not first:
                            pe.wait_ge(exp_done, b * CHUNKS - 3 + i + 1)
                    elif ITEMS[i - 3][0] == "scores":
                        pe.wait_ge(exp_done, b * CHUNKS + ITEMS[i - 3][1] + 1)
                    elif not first:
                        k = ITEMS[i - 3][1]
                        if k < 2:
                            pe.wait_ge(x1_ready, 2 * (b - 1) + k + 1)
                        else:
                            pe.wait_ge((xqT_ready, y_ready)[k - 2], 2 * b)

                def tail_item(last_b, k, slot_no, b):
                    free_slot(b, False, ITEMS.index(("tail", k)))
                    if k < 2:
                        project(last_b, k, 2 * slot_no)
                    elif k == 2:
                        transpose_xq(last_b, 2 * slot_no, 2 * slot_no + 1)
                    else:
                        multiply(last_b, 2 * slot_no, 2 * slot_no + 1)

                pe.sem_inc(pv_done, 2)
                pe.wait_ge(pv_clear, 1)
                pe.wait_ge(pads_in[0], 16)
                pe.wait_ge(pads_in[1], 16)
                batch(0, True)
                with pe.Fori(1, B) as b:
                    batch(b, False)
                weigh(B - 1, G - 1, NB - 1, 0)
                weigh(B - 1, G - 1, NB - 1, 1)
            with pe.Else():
                def heads(b):
                    with pe.Fori(0, H) as h:
                        i = b * H + h
                        pe.wait_ge(g_in, 32 * (i + 1))
                        for t in range(NB):
                            n = i * NB + t
                            pe.wait_ge(g_scores_free, n + 1)
                            for half in range(2):
                                last = nc.tensor.matmul(ps[:, half, :], g_q[:, t * P:(t + 1) * P],
                                                        g_k[:, half * CH:(half + 1) * CH], start=True, stop=True)
                            last.then_inc(g_scores, 1)
                            pe.wait_ge(g_exp, n + 1)
                            for k in range(NB):
                                last = nc.tensor.transpose(ps_all[:, 2 * CH + k * P:2 * CH + (k + 1) * P],
                                                           g_p[:, k * P:(k + 1) * P], eye)
                            last.then_inc(g_tr, 1)
                            pe.wait_ge(g_pT, n + 1)
                            for k in range(NB):
                                last = nc.tensor.matmul(ps[:, 4, 0:VW], g_pT_s[:, k * P:(k + 1) * P],
                                                        V[:, bass.ds(b * NB + k, 1), bass.ds(h, 1), :],
                                                        start=k == 0, stop=k == NB - 1)
                            last.then_inc(g_o, 1)
                    pe.wait_ge(g_norm, (b + 1) * H * NB + 1)
                    for half in range(2):
                        for t in range(4):
                            k = 4 * half + t
                            last = nc.tensor.transpose(ps[:, half, t * P:(t + 1) * P], g_otok[:, k * D:(k + 1) * D], eye)
                        last.then_inc(g_otr, 1)

                with pe.Fori(0, B - 1) as b:
                    heads(b)
                    tail(b)
                heads(B - 1)

            tail(B - 1)

        @block.vector
        def _(dve):
            count = [0]

            def chain(ins):
                count[0] += 1
                ins.then_inc(dve_step, 1)
                dve.wait_ge(dve_step, count[0])

            def inverse_std(lo, n):
                var, y, y2 = rs[:, 0, lo:lo + n], rs[:, 1, lo:lo + n], rs[:, 2, lo:lo + n]
                chain(nc.vector.tensor_scalar(var, mv[:, lo:lo + n, 1], EPS, None, ALU.add))
                chain(nc.vector.tensor_scalar(y2.bitcast(I32), var.bitcast(I32), 1, None, ALU.logical_shift_right))
                chain(nc.vector.tensor_scalar(y.bitcast(I32), y2.bitcast(I32), -1.0, RSQRT_MAGIC, ALU.mult, ALU.add))
                for _ in range(3):
                    chain(nc.vector.tensor_tensor(y2, y, y, ALU.mult))
                    chain(nc.vector.scalar_tensor_tensor(out=y2, in0=y2, scalar=-0.5, in1=var, op0=ALU.mult, op1=ALU.mult))
                    chain(nc.vector.scalar_tensor_tensor(out=y, in0=y2, scalar=1.5, in1=y, op0=ALU.add, op1=ALU.mult))

            def token_stats(src, lo, n):
                for t in range(lo, lo + n):
                    last = nc.vector.bn_stats(stats[:, t, :], src[:, t, :])
                chain(last)
                for t in range(lo, lo + n):
                    last = nc.vector.bn_aggr(mv[:, t, :], stats[:, t, :])
                chain(last)
                inverse_std(lo, n)

            def to_fp8_grid(src, m):
                chain(nc.vector.tensor_scalar(m.bitcast(I32), src.bitcast(I32), 0x7F800000, None, ALU.bitwise_and))
                return nc.vector.tensor_scalar(m, m, 2.0 ** -6, 1.5 * 2.0 ** 20, ALU.max, ALU.mult)

            def overflow_to_nan(dst, r, tmp):
                chain(nc.vector.scalar_tensor_tensor(out=tmp, in0=r, scalar=NAN_SCALE, in1=r, op0=ALU.mult, op1=ALU.mult))
                return nc.vector.scalar_tensor_tensor(out=dst, in0=tmp, scalar=0.0, in1=r, op0=ALU.mult, op1=ALU.add)

            nc.vector.memset(V[:, :, :, HD:VW], 1.0).then_inc(v_ones, 1)
            nc.vector.memset(ones[:, :], 1.0)
            def norm_tiles(lo, n):
                for b in range(lo // NB, (lo + n) // NB):
                    dve.wait_ge(x_in[b], 16)
                token_stats(X, lo, n)
                for t in range(lo, lo + n):
                    last = nc.vector.tensor_scalar(X[:, t, :], X[:, t, :], mv[:, t, 0:1], rs[:, 1, t:t + 1],
                                                   ALU.subtract, ALU.mult)
                    if t % 4 == 3:
                        last.then_inc(xn_ready, 1)

            def split(src, a, v):
                s0 = split_s[:, :]
                out0, out1, out2 = [part(0, a, k, v) for k in range(PARTS)]
                chain(nc.vector.tensor_tensor(s0, src, decay[:, (a + v) % 2, :], ALU.mult))
                chain(nc.vector.tensor_copy(out0, s0))
                chain(nc.vector.tensor_tensor(s0, s0, out0, ALU.subtract))
                chain(nc.vector.tensor_copy(out1, s0))
                chain(nc.vector.tensor_tensor(out2, s0, out1, ALU.subtract))

            norm_tiles(0, NB)
            norm_tiles(NB, (B - 1) * NB)
            dve.wait_ge(c_in, 16)
            dve.wait_ge(q_sb, 2)
            split(qT[:, 0:S], Q, PLUS)
            split(qT[:, 0:S], Q, MINUS)
            dve.sem_inc(q_parts, 1)
            dve.wait_ge(k_sb, 2)
            split(kT[:, 0:S], K, PLUS)
            dve.sem_inc(parts_ready, 1)
            dve.wait_ge(c0_in, 16)
            nc.vector.tensor_copy(hsum[:, :], hsum_f).then_inc(const_ready, 1)

            dve.wait_ge(const_in, 16 * 5)
            chain(nc.vector.reciprocal(rscales[:, :], scales[:, :]))
            chain(nc.vector.tensor_scalar(w8f, w8_s[:, :], rscales[:, 1:2], None, ALU.mult))
            chain(to_fp8_grid(w8f, w8m))
            chain(nc.vector.tensor_tensor(w8f, w8f, w8m, ALU.add))
            chain(nc.vector.tensor_tensor(w8f, w8f, w8m, ALU.subtract))
            nc.vector.tensor_copy(eye16[:, :], eye)
            nc.vector.tensor_tensor(oscale[:, :], scales[:, 0:1], scales[:, 1:2], ALU.mult)
            overflow_to_nan(kq[:, :], w8f, w8m).then_inc(kq_ready, 1)

            dve.wait_ge(norm_ps, 1)
            for i in range(2):
                nc.vector.tensor_reduce(norms[:, i:i + 1], ps_all[:, i * S:(i + 1) * S], AX.X, ALU.max)
                nc.vector.tensor_reduce(norms[:, 2 + i:3 + i], ps_all[:, i * S:(i + 1) * S], AX.X, ALU.add)
            chain(nc.vector.tensor_reduce(norms[:, 5:6], wv_eff[:, :], AX.X, ALU.max, apply_absolute_value=True))
            nc.vector.tensor_scalar(norms[:, 0:1], norms[:, 0:1], norms[:, 1:2], NORM_LIMIT, ALU.mult, ALU.is_le)
            nc.vector.tensor_scalar(norms[:, 2:3], norms[:, 2:3], norms[:, 3:4], 3.0e38, ALU.add, ALU.is_le)
            chain(nc.vector.tensor_scalar(norms[:, 5:6], norms[:, 5:6], VALUE_BOUND / (D * 12.0), None, ALU.is_le))
            chain(nc.vector.tensor_tensor(norms[:, 0:1], norms[:, 0:1], norms[:, 2:3], ALU.mult))
            nc.vector.tensor_tensor(norms[:, 6:7], norms[:, 0:1], norms[:, 5:6], ALU.mult).then_inc(ok_ready, 1)
            dve.wait_ge(ok_ps, 1)
            nc.vector.tensor_scalar(flag[0:1, 0:1], ps[0:1, 4, 0:1], P - 0.5, None, ALU.is_ge).then_inc(flag_ready, 1)

            tail_count = [0]

            def own(ins, b):
                tail_count[0] += 1
                ins.then_inc(tail_step, 1)
                wait(dve, tail_step, TAIL_STEPS * b + tail_count[0])

            def residual(b, half, bank_no):
                if half == 0:
                    wait(dve, x2_in, 16 * b + 16)
                wait(dve, proj_ps, 2 * b + half + 1)
                cols = halves[half]
                nc.vector.tensor_tensor(X1[:, cols], bank(bank_no), X1[:, cols], ALU.add).then_inc(x1_ready, 1)

            def tile_stats(tiles):
                for t in tiles:
                    last = nc.vector.bn_stats(stats[:, t, :], X1[:, t * D:(t + 1) * D])
                return last

            def gather_stats():
                for t in range(NB):
                    last = nc.vector.bn_aggr(mv[:, t, :], stats[:, t, :])
                return last

            def inverse_std_step(i):
                var, y, y2 = [rs[:, k, 0:NB] for k in range(3)]
                if i == 0:
                    return nc.vector.tensor_scalar(var, mv[:, 0:NB, 1], EPS, None, ALU.add)
                if i == 1:
                    return nc.vector.tensor_scalar(y2.bitcast(I32), var.bitcast(I32), 1, None, ALU.logical_shift_right)
                if i == 2:
                    return nc.vector.tensor_scalar(y.bitcast(I32), y2.bitcast(I32), -1.0, RSQRT_MAGIC, ALU.mult, ALU.add)
                if i % 3 == 0:
                    return nc.vector.tensor_tensor(y2, y, y, ALU.mult)
                if i % 3 == 1:
                    return nc.vector.scalar_tensor_tensor(out=y2, in0=y2, scalar=-0.5, in1=var, op0=ALU.mult, op1=ALU.mult)
                return nc.vector.scalar_tensor_tensor(out=y, in0=y2, scalar=1.5, in1=y, op0=ALU.add, op1=ALU.mult)

            def normalise_tiles(tiles):
                for t in tiles:
                    last = nc.vector.tensor_scalar(xn2[:, t * D:(t + 1) * D], X1[:, t * D:(t + 1) * D], mv[:, t, 0:1],
                                                   rs[:, 1, t:t + 1], ALU.subtract, ALU.mult)
                return last

            def divide(half):
                return nc.vector.tensor_scalar(xs[:, halves[half]], xn2[:, halves[half]], rscales[:, 0:1], None, ALU.mult)

            def grid_step(b, half):
                x_h, m_h = xs[:, halves[half]], magic[:, halves[half]]
                own(nc.vector.tensor_scalar(m_h.bitcast(I32), x_h.bitcast(I32), 0x7F800000, None, ALU.bitwise_and), b)
                nc.vector.tensor_scalar(m_h, m_h, 2.0 ** -6, 1.5 * 2.0 ** 20, ALU.max, ALU.mult).then_inc(magic_ready, 1)

            def quantised(b, half, step):
                x_h, m_h = xs[:, halves[half]], magic[:, halves[half]]
                if step == 0:
                    wait(dve, rounded, 2 * b + half + 1)
                    own(nc.vector.scalar_tensor_tensor(out=m_h, in0=x_h, scalar=NAN_SCALE, in1=x_h, op0=ALU.mult,
                                                       op1=ALU.mult), b)
                else:
                    nc.vector.scalar_tensor_tensor(out=xq[:, halves[half]], in0=m_h, scalar=0.0, in1=x_h, op0=ALU.mult,
                                                   op1=ALU.add).then_inc(xq_ready, 1)

            def add_bias(half):
                y3 = yb[:, halves[half]].rearrange("p (t d) -> p t d", d=D)
                return nc.vector.tensor_tensor(y3, y3, bias_s[:, :].rearrange("p (o d) -> p o d", o=1)
                                               .broadcast_to([P, 4, D]), ALU.add)

            def result(half):
                cols = halves[half]
                nc.vector.tensor_tensor(X1[:, cols], X1[:, cols], yb[:, cols], ALU.add).then_inc(res_ready, 1)

            def tail_piece(b, c):
                i, odd = c // 2 - 1, c % 2
                if c == XQT_CHUNK or c == XQT_CHUNK + 1:
                    half = c - XQT_CHUNK
                    wait(dve, xqT_ps, 2 * b + 2)
                    nc.vector.tensor_copy(xqT[:, halves[half]],
                                          bank16(2 * slot(*INSERTED[2], True) + half)).then_inc(xqT_ready, 1)
                elif c == Y_CHUNK or c == Y_CHUNK + 1:
                    half = c - Y_CHUNK
                    wait(dve, y_ps, 2 * b + 2)
                    nc.vector.tensor_scalar(yb[:, halves[half]], bank(2 * slot(*INSERTED[3], True) + half),
                                            oscale[:, 0:1], None, ALU.mult).then_inc(y_ready, 1)
                elif odd or i < 0:
                    return
                elif i < 2:
                    residual(b, i, 2 * slot(*INSERTED[i], True))
                elif i == 2:
                    wait(dve, x1_ready, 2 * b + 2)
                    tile_stats((0, 1))
                elif i < 5:
                    tile_stats((2 * i - 4, 2 * i - 3))
                elif i == 5:
                    own(tile_stats((6, 7)), b)
                elif i == 6:
                    own(gather_stats(), b)
                elif i < 13:
                    for step in (2 * i - 14, 2 * i - 13):
                        own(inverse_std_step(step), b)
                elif i < 16:
                    normalise_tiles((2 * i - 26, 2 * i - 25))
                elif i == 16:
                    own(normalise_tiles((6, 7)), b)
                elif i < 19:
                    own(divide(i - 17), b)
                    grid_step(b, i - 17)
                elif 24 <= i < 28:
                    quantised(b, (i - 24) // 2, i % 2)
                elif c == Y_CHUNK + 2:
                    wait(dve, y_ready, 2 * b + 2)
                    add_bias(0)
                    own(add_bias(1), b)
                elif c == Y_CHUNK + 4:
                    result(0)
                elif c == Y_CHUNK + 6:
                    result(1)

            def tail(b):
                tail_count[0] = 0
                residual(b, 0, 2)
                residual(b, 1, 3)
                wait(dve, x1_ready, 2 * b + 2)
                own(tile_stats(range(NB)), b)
                own(gather_stats(), b)
                for step in range(12):
                    own(inverse_std_step(step), b)
                for half in range(2):
                    own(normalise_tiles(range(4 * half, 4 * half + 4)), b)
                    own(divide(half), b)
                    grid_step(b, half)
                for half in range(2):
                    quantised(b, half, 0)
                    quantised(b, half, 1)
                for half in range(2):
                    wait(dve, y_ready, 2 * b + half + 1)
                    own(add_bias(half), b)
                    result(half)
                pad_steps(b)

            def pad_steps(b):
                assert tail_count[0] <= TAIL_STEPS
                if tail_count[0] < TAIL_STEPS:
                    dve.sem_inc(tail_step, TAIL_STEPS - tail_count[0])
                tail_count[0] = 0

            dve.wait_ge(flag_ready, 1)
            bounded = dve.value_load(flag[0:1, 0:1], min_val=0, max_val=1)
            with dve.If(bounded > 0):
                nc.vector.memset(pv, 0.0).then_inc(pv_clear, 1)
                dve.sem_inc(pv_copied, 2)

                def copy_pv(group, half, first):
                    if half == 0:
                        dve.wait_ge(pv_first, NB * (group + 1))
                        if not first:
                            dve.wait_ge(out_moved, 16 * 2 * HG * group)
                    else:
                        dve.wait_ge(pv_done, NB * (group + 1) + 2)
                    nc.vector.tensor_copy(pv_out[0:96 + VW, halves[half]],
                                          pv[0:96 + VW, halves[half]]).then_inc(pv_copied, 1)

                def invert_sums(b, half):
                    if half == 0:
                        dve.wait_ge(out_moved, 16 * 2 * HG * G * (b + 1))
                    part = slice(half * (S // HD // 2), (half + 1) * (S // HD // 2))
                    nc.vector.reciprocal(rec[:, part], den[:, part]).then_inc(rec_ready, 1)

                def batch(b, first):
                    for hg in range(G):
                        for m in range(NB * HG):
                            kc, j = m // HG, m % HG
                            dve.wait_ge(edge_ready, (b * G + hg) * NB * HG + m + 1)
                            own = score[slot(hg, m)][:, kc * P:(kc + 1) * P]
                            nc.vector.tensor_tensor(own, own, fix, ALU.mult).then_inc(diag_fixed, 1)
                            if m in (2, 4) and not (first and hg == 0):
                                copy_pv(b * G + hg - 1, m // 2 - 1, first and hg == 1)
                            if hg == 0 and m in (14, 16) and not first:
                                invert_sums(b - 1, m // 2 - 7)
                            if hg > 0 and not first:
                                tail_piece(b - 1, (hg - 1) * NB * HG + m)
                    if not first:
                        pad_steps(b - 1)

                batch(0, True)
                with dve.Fori(1, B) as b:
                    batch(b, False)
                copy_pv(B * G - 1, 0, False)
                copy_pv(B * G - 1, 1, False)
                invert_sums(B - 1, 0)
                invert_sums(B - 1, 1)
            with dve.Else():
                dve.sem_inc(g_scores_free, 1)
                dve.sem_inc(g_norm, 1)
                dve.wait_ge(g_table, 16)
                def heads(b):
                    with dve.Fori(0, H) as h:
                        for t in range(NB):
                            n = (b * H + h) * NB + t
                            done = 4 * n
                            dve.wait_ge(g_scores, n + 1)
                            nc.vector.tensor_scalar(g_clip, ps_all[:, 0:S], SCALE, -CLAMP, ALU.mult, ALU.max).then_inc(g_step, 1)
                            dve.wait_ge(g_step, done + 1)
                            dve.sem_inc(g_scores_free, 1)
                            u0 = S - P - t * P
                            nc.vector.scalar_tensor_tensor(out=g_dec_s, in0=g_clip, scalar=CLAMP,
                                                           in1=g_table_s[:, u0:u0 + S], op0=ALU.min,
                                                           op1=ALU.mult).then_inc(g_step, 1)
                            dve.wait_ge(g_step, done + 2)
                            nc.vector.tensor_reduce(norms[:, 6:7], g_dec_s, AX.X, ALU.max).then_inc(g_step, 1)
                            dve.wait_ge(g_step, done + 3)
                            nc.vector.tensor_scalar(norms[:, 7:8], norms[:, 6:7], -1.0, None, ALU.mult).then_inc(g_max, 1)
                            dve.wait_ge(g_tr, n + 1)
                            nc.vector.tensor_copy(g_pT_s, ps_all[:, 2 * CH:2 * CH + S]).then_inc(g_pT, 1)
                            dve.wait_ge(g_o, n + 1)
                            nc.vector.reciprocal(norms[:, 5:6], ps[:, 4, HD:VW]).then_inc(g_step, 1)
                            dve.wait_ge(g_step, done + 4)
                            nc.vector.tensor_scalar(g_otok[:, bass.ds(t * D + h * HD, HD)], ps[:, 4, 0:HD],
                                                    norms[:, 5:6], None, ALU.mult).then_inc(g_norm, 1)

                with dve.Fori(0, B - 1) as b:
                    heads(b)
                    tail(b)
                heads(B - 1)

            tail(B - 1)


_INS = ['L0_attn_x', 'L0_attn_Wq', 'L0_attn_Wk', 'L0_attn_Wv', 'L0_attn_Wo', 'L0_attn_W_down_kv', 'L0_attn_W_up_k',
        'L0_attn_W_up_v', 'L0_ffn_kernel', 'L0_ffn_input_scale', 'L0_ffn_kernel_scale', 'L0_ffn_bias']


def constants():
    import numpy as np
    c = 0.01 * 0.01
    i = np.arange(S, dtype=np.float64)
    rows = np.concatenate([np.exp(-c * i), np.exp(c * i)])[None, :]
    p = np.arange(P)[:, None]
    table = np.exp(-c * np.abs(p - np.arange(TABLE)[None, :] + S - P))
    key, query = p, np.arange(P)[None, :]
    fix = np.exp(-2 * c * np.maximum(key - query, 0))
    head_sum = (np.arange(P)[:, None] // HD == np.arange(32)[None, :]).astype(np.float64)
    return {"decay_rows": rows, "decay_table": table, "const_cols": np.concatenate([np.eye(P), fix, head_sum], 1),
            "zeros": np.zeros((1, HG * 2 * S))}


def kernel(**inputs):
    import numpy as np
    import concourse.bacc as bacc
    from concourse.bass_utils import run_bass_kernel_spmd

    nc = bacc.Bacc("TRN2", target_bir_lowering=False, num_devices=1)
    arrays = {}
    for name in _INS:
        a = np.ascontiguousarray(inputs[name])
        if a.ndim == 3:
            a = a.reshape(B * S, D)
        if a.ndim == 1:
            a = a.reshape(1, -1)
        arrays[name] = a
    for name, a in constants().items():
        arrays[name] = np.ascontiguousarray(a.astype(np.float32))
    args = [nc.dram_tensor(n, a.shape, mybir.dt.from_np(a.dtype), kind="ExternalInput").ap() for n, a in arrays.items()]
    out = nc.dram_tensor("out", (B * S, D), F32, kind="ExternalOutput").ap()
    qt_dram = nc.dram_tensor("qt_dram", (P, B * S), F32, kind="Internal").ap()
    kt_dram = nc.dram_tensor("kt_dram", (P, B * S), F32, kind="Internal").ap()
    v_dram = nc.dram_tensor("v_dram", (P, NT * H * VW), F32, kind="Internal").ap()
    rec_dram = nc.dram_tensor("rec_dram", (H, S), F32, kind="Internal").ap()
    build(nc, *args, out, qt_dram, kt_dram, v_dram, rec_dram)
    r = run_bass_kernel_spmd(nc, [arrays], core_ids=[0])
    return r.results[0]["out"].reshape(B, S, D)
```

```python
import concourse.bass as bass
from concourse import mybir
from contextlib import ExitStack

F32 = mybir.dt.float32
BF16 = mybir.dt.bfloat16
I32 = mybir.dt.int32
ALU = mybir.AluOpType
ACT = mybir.ActivationFunctionType
AX = mybir.AxisListType

B, S, D = 4, 1024, 128
H, HD = 16, 8
DL = 32
P = 128
NT = B * S // P
NB = S // P
HG = 4
G = H // HG
CH = 512
NC = B * S // CH
PARTS = 3
ROWS = HD * PARTS * PARTS
KROWS = 96
VB = NB * H * (HD + 1)
VW = HD + 1
FILL = 16 * 2 * PARTS * HG
SCALE = 1.0 / (float(D) ** 0.5 + 1e-8)
CLAMP = 10000.0
EPS = 1e-5
SCORE_BOUND = 40.0
VALUE_BOUND = 1e16
NORM_LIMIT = (SCORE_BOUND / SCALE) ** 2 / 1.02
Q, K = range(2)
PLUS, MINUS = range(2)
NAN_SCALE = 3.0e38 / (464.0 * 464.0)
TABLE = 2 * S - P
RSQRT_MAGIC = float(0x5F3759DF)

JOBS = [("T", 0)]
for _c in range(NC):
    JOBS += [("T", _c + 1)] * (_c + 1 < NC) + [("q", _c), ("k", _c)] + [("v", _c)] * (_c < 2)
LATE_V = range(2, NC)
V_BANKS = (5, 6, 7)

CHUNKS = G * NB * HG
INSERTED = [(1, 8), (1, 10), (3, 8), (3, 16)]
ITEMS = []
for _hg in range(G):
    for _m in range(NB * HG):
        if (_hg, _m) in INSERTED:
            ITEMS.append(("tail", INSERTED.index((_hg, _m))))
        ITEMS.append(("scores", _hg * NB * HG + _m))
XQT_CHUNK, Y_CHUNK = [(_hg - 1) * NB * HG + _m for _hg, _m in INSERTED[2:]]
PIECES = [_c for _c in range(INSERTED[0][1], 3 * NB * HG, 2) if _c % (NB * HG) not in (4, 6)]
TAIL_STEPS = 24
assert len(ITEMS) % 3 == 0


def item(hg, m):
    return ITEMS.index(("scores", hg * NB * HG + m))


def slot(hg, m, inserted=False, first=False):
    if first:
        return (hg * NB * HG + m + 1) % 3
    return (item(hg, m) - inserted) % 3


def build(nc, x, wq, wk, wv, wo, wd, wuk, wuv, w8, s_in, s_k, bias, decay_rows, decay_table,
          const_cols, zeros, out, qt_dram, kt_dram, v_dram, rec_dram):
    with ExitStack() as ctx:
        def sb(name, shape, dt=F32):
            return ctx.enter_context(nc.sbuf_tensor(name, shape, dt))

        def sem(name):
            return ctx.enter_context(nc.semaphore(name))

        late1 = sb("late1", [P, 4 * S])
        late2 = sb("late2", [P, 4, S])
        OT = sb("OT", [P, S])
        Vb = sb("Vb", [P, NB, H, VW])
        qk_b = late2[:, 0:2, :]
        stage = sb("stage", [P, 2, HG, 2, 2, S], BF16)
        probs = sb("probs", [P, 2 * HG, S])
        parts = sb("parts", [P, 2, 2 * PARTS * 2 * S], BF16)
        pv_out = sb("pv_out", [P, S])
        o_raw = late2[:, 2, :]
        rec_b = late2[:, 3, :]
        den = sb("den", [P, S // HD])
        rec = sb("rec", [P, S // HD])
        decay = sb("decay", [P, 2, S])
        split_s = sb("split_s", [P, S])
        consts = sb("consts", [P, 3 * P + HD + 32])
        eye, fix, hsum_f = consts[:, 0:P], consts[:, P:2 * P], consts[:, 2 * P:2 * P + 32]
        same_head = consts[:, 2 * P + 32:3 * P + 32]
        place = consts[:, 3 * P + 32:3 * P + 32 + HD]
        eye16 = sb("eye16", [P, P], BF16)
        hsum = sb("hsum", [P, 32], BF16)
        wq_s = sb("wq_s", [P, D])
        wo_s = sb("wo_s", [P, D])
        wk_eff = sb("wk_eff", [P, D])
        wv_eff = sb("wv_eff", [P, D])
        w8_s = sb("w8_s", [P, D], BF16)
        kq = sb("kq", [P, D], BF16)
        bias_s = sb("bias_s", [P, D], BF16)
        scales = sb("scales", [P, 2])
        rscales = sb("rscales", [P, 2])
        oscale = sb("oscale", [P, 1])
        stats = sb("stats", [P, NT, 6])
        mv = sb("mv", [P, NT, 2])
        rs = sb("rs", [P, 3, NT])
        norms = sb("norms", [P, 8])
        flag = sb("flag", [1, 1], I32)
        ones = sb("ones", [P, 1])

        X = probs[:, 0:HG, :].rearrange("p a (t d) -> p (a t) d", d=D)
        xnT = probs[:, HG:2 * HG, :].rearrange("p a n -> p (a n)")
        qT, kT = late1[:, :], late2[:, :, :].rearrange("p a n -> p (a n)")

        second = stage[:, 1, :, :, :, :].rearrange("p j a v n -> p (j a v n)")

        def squares(which, c):
            return second[:, (which * NC + c) * CH:(which * NC + c + 1) * CH]

        V = parts[:, 1, :].bitcast(F32)[:, 0:NT * H * VW].rearrange("p (t h w) -> p t h w", t=NT, h=H)

        def part(buf, a, k, v=None):
            at = (a * PARTS + k) * 2 * S
            return parts[:, buf, at:at + 2 * S] if v is None else parts[:, buf, at + v * S:at + (v + 1) * S]

        wk_s, wv_s, wkv_T = [pv_out[:, i * D:(i + 1) * D] for i in range(3)]
        wuk_s, wuv_s, wdown_T = [pv_out[0:DL, i * D:(i + 1) * D] for i in range(3, 6)]
        wd_s = pv_out[:, 6 * D:6 * D + DL]
        gen = stage[:, :, :, :, :, :].rearrange("p u j a v n -> p (u j a v n)").bitcast(F32)
        g_clip, g_dec_s, g_p, g_pT_s = [gen[:, i * S:(i + 1) * S] for i in range(4)]
        g_otok = gen[:, 4 * S:5 * S]
        g_table_s = gen[:, 8 * S:8 * S + TABLE]
        g_q, g_k = gen[0:HD, 10 * S:11 * S], gen[0:HD, 11 * S:12 * S]

        ps = ctx.enter_context(nc.psum_tensor("ps", [P, 8, CH], F32))
        ps_all = ps[:, :, :].rearrange("p b n -> p (b n)")
        score = [ps_all[:, i * S:(i + 1) * S] for i in range(3)]
        pv = ps_all[:, 6 * CH:8 * CH]

        x_in = [sem(f"x_in{b}") for b in range(B)]
        w_in = sem("w_in")
        wq_in = sem("wq_in")
        tables_in = sem("tables_in")
        decay_in = sem("decay_in")
        waited = sem("waited")
        const_in = sem("const_in")
        fold_w_in = sem("fold_w_in")
        kq_ready = sem("kq_ready")
        pv_clear = sem("pv_clear")
        g_ot = sem("g_ot")
        dve_step = sem("dve_step")
        pool_split = sem("pool_split")
        pool_tail = sem("pool_tail")
        wkv_ready = sem("wkv_ready")
        fold_pe = sem("fold_pe")
        fold_act = sem("fold_act")
        xn_ready = sem("xn_ready")
        tr_ready = sem("tr_ready")
        xnT_ready = sem("xnT_ready")
        q_ps = sem("q_ps")
        k_ps = sem("k_ps")
        v_ps = sem("v_ps")
        q_sb = sem("q_sb")
        k_sb = sem("k_sb")
        v_sb = sem("v_sb")
        v_ones = sem("v_ones")
        stats_ready = sem("stats_ready")
        centred = sem("centred")
        q_parts = sem("q_parts")
        pv_first = sem("pv_first")
        norm_ps = sem("norm_ps")
        ok_ready = sem("ok_ready")
        ok_ps = sem("ok_ps")
        flag_ready = sem("flag_ready")
        const_ready = sem("const_ready")
        parts_ready = sem("parts_ready")
        vb_in = [sem(f"vb_in{hg}") for hg in range(G)]
        qk_in = sem("qk_in")
        dram_out = sem("dram_out")
        pads_in = [sem(f"pads_in{u}") for u in range(2)]
        late_k_in = [sem(f"late_k_in{j}") for j in (2, 3)]
        head_in = [sem(f"head_in{j}") for j in range(HG)]
        stage_in = [sem(f"stage_in{u}") for u in range(2)]
        edge_ready = sem("edge_ready")
        diag_fixed = sem("diag_fixed")
        qk_done = sem("qk_done")
        exp_done = sem("exp_done")
        pv_done = sem("pv_done")
        pv_copied = sem("pv_copied")
        out_moved = sem("out_moved")
        sums_moved = sem("sums_moved")
        rec_ready = sem("rec_ready")
        rec_stored = sem("rec_stored")
        rec_in = sem("rec_in")
        spread = sem("spread")
        spread_ps = sem("spread_ps")
        ot_ready = sem("ot_ready")
        g_table = sem("g_table")
        g_in = sem("g_in")
        g_step = sem("g_step")
        g_scores = sem("g_scores")
        g_scores_free = sem("g_scores_free")
        g_max = sem("g_max")
        g_exp = sem("g_exp")
        g_tr = sem("g_tr")
        g_pT = sem("g_pT")
        g_o = sem("g_o")
        g_norm = sem("g_norm")
        g_otr = sem("g_otr")
        x2_in = sem("x2_in")
        scaled = sem("scaled")
        tail_step = sem("tail_step")
        proj_ps = sem("proj_ps")
        x1_ready = sem("x1_ready")
        ln2_ready = sem("ln2_ready")
        magic_ready = sem("magic_ready")
        rounded = sem("rounded")
        xq_ready = sem("xq_ready")
        xqT_ps = sem("xqT_ps")
        xqT_ready = sem("xqT_ready")
        y_ps = sem("y_ps")
        y_ready = sem("y_ready")
        res_ready = sem("res_ready")
        stored = sem("stored")

        block = ctx.enter_context(nc.Block())

        X1 = late1[:, 0:S]
        xs = late1[:, S:2 * S]
        magic = late1[:, 2 * S:3 * S]
        xn2 = late1[:, 3 * S:4 * S].bitcast(BF16)[:, 0:S]
        xq = xn2
        xqT = late1[:, 3 * S:4 * S].bitcast(BF16)[:, S:2 * S]
        yb = xqT
        w8f, w8m = xs[:, 0:D], magic[:, 0:D]
        halves = [slice(half * CH, (half + 1) * CH) for half in range(2)]

        def bank(n):
            return ps[:, n, :]

        def bank16(n):
            return ps[:, n, :].bitcast(BF16)[:, 0:CH]

        def wait(engine, semaphore, value):
            engine.wait_ge(semaphore, value)
            if not isinstance(value, int):
                engine.sem_inc(waited, 1)

        @block.sync
        def _(sp):
            x_t = x.rearrange("(t p) d -> p t d", p=P)
            for b in range(B):
                sp.dma_start(X[:, b * NB:(b + 1) * NB, :], x_t[:, b * NB:(b + 1) * NB, :]).then_inc(x_in[b], 16)
                if b == 0:
                    sp.dma_start(wq_s[:, :], wq[:, :]).then_inc(wq_in, 16)
                    sp.dma_start(decay[:, :, :].rearrange("p a n -> p (a n)"),
                                 decay_rows.broadcast_to([P, 2 * S])).then_inc(decay_in, 16)

            def clear_pads(u):
                n = KROWS - ROWS
                sp.dma_start(stage[ROWS:KROWS, u, :, :, :, :].rearrange("p j a v n -> p (j a v n)").bitcast(F32),
                             zeros.broadcast_to([n, HG * 2 * S])).then_inc(pads_in[u], 16)

            def stage_group(b, hg, u, buf, which=(Q, K), js=range(HG)):
                if js[0] == 0 and not (isinstance(b, int) and b == 0 and hg < 2):
                    wait(sp, qk_done, HG * NB * (b * G + hg - 1))
                for j in js:
                    h = hg * HG + j
                    heads = slice(HD * h, HD * h + HD)
                    for k in range(PARTS):
                        rows = slice(k, ROWS, PARTS)
                        all_q = parts[heads, buf, 0:PARTS * 2 * S].rearrange("p (k n) -> p k n", k=PARTS)
                        at = (PARTS + k) * 2 * S
                        k_part = parts[heads, buf, at:at + 2 * S].rearrange("p (o n) -> p o n", o=1)
                        for a in which:
                            src = (all_q, k_part.broadcast_to([HD, PARTS, 2 * S]))[a]
                            very_first = isinstance(b, int) and b == 0 and hg == 0
                            sp.dma_start(stage[rows, u, j, a, :, :].rearrange("p v n -> p (v n)"),
                                         src).then_inc(head_in[j] if very_first else stage_in[u], 16)

            clear_pads(0)

            def store_v(b):
                sp.wait_ge(v_sb, 2 * b + 2)
                sp.dma_start(v_dram[:, b * VB:(b + 1) * VB],
                             V[:, b * NB:(b + 1) * NB, :, :].rearrange("p t h w -> p (t h w)")).then_inc(dram_out, 16)

            sp.wait_ge(v_ones, 1)
            for b in range(B):
                cols = slice(b * S, (b + 1) * S)
                sp.wait_ge(q_sb, 2 * b + 2)
                sp.dma_start(qt_dram[:, cols], qT[:, cols]).then_inc(dram_out, 16)
                sp.wait_ge(k_sb, 2 * b + 2)
                sp.dma_start(kt_dram[:, cols], kT[:, cols]).then_inc(dram_out, 16)
                if b == 0:
                    store_v(0)
                    for hg in range(G):
                        heads = slice(hg * HG, (hg + 1) * HG)
                        sp.dma_start(Vb[:, :, heads, :].rearrange("p t h w -> p t (h w)"),
                                     V[:, 0:NB, heads, :].rearrange("p t h w -> p t (h w)")).then_inc(vb_in[hg], 16)
            sp.wait_ge(q_parts, 1)
            stage_group(0, 0, 0, 0, (Q,), js=(0, 1))
            sp.wait_ge(parts_ready, 2)
            stage_group(0, 0, 0, 0, (K,), js=(0, 1))
            stage_group(0, 0, 0, 0, (Q,), js=(2, 3))
            sp.wait_ge(norm_ps, 1)
            clear_pads(1)
            stage_group(0, 1, 1, 0)
            for b in range(1, B):
                store_v(b)
            sp.wait_ge(dram_out, 16 * 3 * B)

            def load_x(b):
                sp.dma_start(X1.rearrange("p (t d) -> p t d", d=D),
                             x[bass.ds(b * S, S), :].rearrange("(t p) d -> p t d", p=P)).then_inc(x2_in, 16)

            def store_result(b):
                wait(sp, res_ready, 2 * b + 2)
                sp.dma_start(out[bass.ds(b * S, S), :].rearrange("(t p) d -> p t d", p=P),
                             X1.rearrange("p (t d) -> p t d", d=D)).then_inc(stored, 16)
                wait(sp, stored, 16 * b + 16)

            sp.wait_ge(flag_ready, 1)
            bounded = sp.value_load(flag[0:1, 0:1], min_val=0, max_val=1)
            with sp.If(bounded > 0):
                def load_values(b, hg):
                    heads = slice(hg * HG, (hg + 1) * HG)
                    sp.dma_start(Vb[:, :, heads, :].rearrange("p t h w -> p t (h w)"),
                                 v_dram[:, bass.ds(b * VB, VB)].rearrange("p (t h w) -> p t h w", t=NB, h=H)
                                 [:, :, heads, :].rearrange("p t h w -> p t (h w)")).then_inc(vb_in[hg], 16)

                def load_qk(b):
                    for a, src in ((Q, qt_dram), (K, kt_dram)):
                        sp.dma_start(qk_b[:, a, :], src[:, bass.ds(b * S, S)]).then_inc(qk_in, 16)

                def store_group(b, hg):
                    wait(sp, pv_copied, 2 * (b * G + hg + 2))
                    for j in range(HG):
                        h = hg * HG + j
                        sp.dma_start(den[HD * h:HD * h + HD, :],
                                     pv_out[32 * j + HD:32 * j + HD + 1, :].rearrange("p (c t) -> p c t", c=HD)
                                     ).then_inc(sums_moved, 16)
                    for j in range(HG):
                        h = hg * HG + j
                        sp.dma_start(o_raw[HD * h:HD * h + HD, :], pv_out[32 * j:32 * j + HD, :]).then_inc(out_moved, 16)

                def batch(b, first, last):
                    for hg in range(G):
                        if hg == 0:
                            if not last:
                                load_qk(b + 1)
                        if hg == 2 and not last:
                            wait(sp, stage_in[0], FILL * (2 * b + 2))
                            wait(sp, stage_in[1], FILL * (2 * b + 2))
                            wait(sp, parts_ready, 2 * b + 4)
                        if hg == G - 1:
                            if not first:
                                store_result(b - 1)
                            load_x(b)
                        for js in ((0, 1), (2, 3)):
                            if hg < 2:
                                stage_group(b, hg + 2, hg % 2, b % 2, js=js)
                            elif not last:
                                stage_group(b + 1, hg - 2, hg % 2, (b + 1) % 2, js=js)
                            if js[0] == 0:
                                if hg == 0 and not first:
                                    wait(sp, ot_ready, b)
                                store_group(b, hg)
                        if not last:
                            load_values(b + 1, hg)

                batch(0, True, False)
                with sp.Fori(1, B - 1) as b:
                    batch(b, False, False)
                batch(B - 1, False, True)
            with sp.Else():
                for j in (2, 3):
                    wait(sp, late_k_in[j - 2], FILL // HG // 2)
                for j in range(HG):
                    wait(sp, head_in[j], FILL // HG // (1 + (j >= 2)))
                wait(sp, stage_in[1], FILL)
                wait(sp, pads_in[0], 16)
                wait(sp, pads_in[1], 16)
                sp.dma_start(g_table_s, decay_table[:, :]).then_inc(g_table, 16)

                def heads(b):
                    with sp.Fori(0, H) as h:
                        wait(sp, g_norm, (b * H + h) * NB + 1)
                        sp.dma_start(g_q, qt_dram[bass.ds(h * HD, HD), bass.ds(b * S, S)]).then_inc(g_in, 16)
                        sp.dma_start(g_k, kt_dram[bass.ds(h * HD, HD), bass.ds(b * S, S)]).then_inc(g_in, 16)

                with sp.Fori(0, B - 1) as b:
                    heads(b)
                    load_x(b)
                    store_result(b)
                heads(B - 1)
                load_x(B - 1)

            for half in range(2):
                sp.wait_ge(res_ready, 2 * B - 1 + half)
                rows = slice((B - 1) * S + half * CH, (B - 1) * S + (half + 1) * CH)
                sp.dma_start(out[rows, :].rearrange("(t p) d -> p t d", p=P),
                             X1[:, halves[half]].rearrange("p (t d) -> p t d", d=D)).then_inc(stored, 16)
            sp.wait_ge(stored, 16 * (B + 1))

        @block.gpsimd
        def _(pool):
            pool.wait_ge(w_in, 16 * 2)
            nc.gpsimd.tensor_tensor(wk_s, wk_s, wv_s, ALU.add).then_inc(wkv_ready, 1)

            def split(buf, src, a, v, scratch, done):
                row = decay[:, (a + v) % 2, :]
                out0, out1, out2 = [parts[:, buf, (a * PARTS + k) * 2 * S + v * S:(a * PARTS + k) * 2 * S + (v + 1) * S]
                                    for k in range(PARTS)]
                for i, (dst, x0, x1, op) in enumerate(((scratch, src, row, ALU.mult), (out0, src, row, ALU.mult),
                                                       (scratch, scratch, out0, ALU.subtract),
                                                       (out1, scratch, out0, None),
                                                       (out2, scratch, out1, ALU.subtract))):
                    ins = nc.gpsimd.tensor_copy(dst, x0) if op is None else nc.gpsimd.tensor_tensor(dst, x0, x1, op)
                    ins.then_inc(pool_split, 1)
                    wait(pool, pool_split, done + i + 1)

            def normalise_x(i):
                tiles = slice(4 * i, 4 * i + 4)
                x4 = X[:, tiles, :]
                mean = mv[:, tiles, 0:1].broadcast_to([P, 4, D])
                istd = rs[:, 1, tiles].rearrange("p (t o) -> p t o", o=1).broadcast_to([P, 4, D])
                nc.gpsimd.tensor_tensor(x4, x4, mean, ALU.subtract).then_inc(centred, 1)
                pool.wait_ge(centred, i - 5)
                nc.gpsimd.tensor_tensor(x4, x4, istd, ALU.mult).then_inc(xn_ready, 1)

            pool.wait_ge(stats_ready, 1)
            pool.wait_ge(xn_ready, 6)
            for i in range(6, 8):
                normalise_x(i)
            pool.wait_ge(decay_in, 16)
            pool.wait_ge(k_sb, 2)
            split(0, kT[:, 0:S], K, MINUS, pv_out[:, :], 0)
            pool.sem_inc(parts_ready, 1)

            def to_grid(b, half):
                cols = halves[half]
                wait(pool, magic_ready, 2 * b + half + 1)
                nc.gpsimd.tensor_tensor(xs[:, cols], xs[:, cols], magic[:, cols], ALU.add).then_inc(pool_tail, 1)
                wait(pool, pool_tail, 2 * b + half + 1)
                nc.gpsimd.tensor_tensor(xs[:, cols], xs[:, cols], magic[:, cols], ALU.subtract).then_inc(rounded, 1)

            pool.wait_ge(parts_ready, 2)
            for j in (2, 3):
                for k in range(PARTS):
                    k_part = part(0, K, k)[HD * j:HD * j + HD, :].rearrange("p (o n) -> p o n", o=1)
                    pool.dma_start(stage[k:ROWS:PARTS, 0, j, K, :, :].rearrange("p v n -> p (v n)"),
                                   k_part.broadcast_to([HD, PARTS, 2 * S])).then_inc(late_k_in[j - 2], 16)

            pool.wait_ge(flag_ready, 1)
            bounded = pool.value_load(flag[0:1, 0:1], min_val=0, max_val=1)
            with pool.If(bounded > 0):
                def normalise(b):
                    wait(pool, rec_ready, 2 * b + 2)
                    pool.dma_start(rec_dram.rearrange("h (c t) -> (h c) t", c=HD), rec[:, :]).then_inc(rec_stored, 16)
                    wait(pool, rec_stored, 16 * b + 16)
                    pool.dma_start(rec_b, rec_dram.rearrange("h (o n) -> h o n", o=1).broadcast_to([H, HD, S])
                                   ).then_inc(rec_in, 16)
                    wait(pool, out_moved, 16 * HG * G * (b + 1))
                    wait(pool, rec_in, 16 * b + 16)
                    nc.gpsimd.tensor_tensor(OT[:, :], o_raw, rec_b, ALU.mult).then_inc(ot_ready, 1)

                def split_next(b, buf, i):
                    a, v = ((Q, PLUS), (Q, MINUS), (K, PLUS), (K, MINUS))[i]
                    split(buf, qk_b[:, a, :], a, v, split_s[:, :], 5 + 20 * b + 5 * i)

                wait(pool, parts_ready, 2)
                wait(pool, qk_in, 32)
                for i in range(4):
                    split_next(0, 1, i)
                pool.sem_inc(parts_ready, 2)
                with pool.Fori(1, B - 1) as b:
                    normalise(b - 1)
                    wait(pool, qk_in, 32 * (b + 1))
                    for i in range(3):
                        split_next(b, (b + 1) % 2, i)
                    to_grid(b - 1, 0)
                    to_grid(b - 1, 1)
                    split_next(b, (b + 1) % 2, 3)
                    pool.sem_inc(parts_ready, 2)
                normalise(B - 2)
                to_grid(B - 2, 0)
                to_grid(B - 2, 1)
            with pool.Else():
                with pool.Fori(0, B - 1) as b:
                    to_grid(b, 0)
                    pool.sem_inc(pool_tail, 1)

            to_grid(B - 1, 0)

        @block.scalar
        def _(act):
            act.dma_start(wk_s, wk[:, :]).then_inc(w_in, 16)
            act.dma_start(wv_s, wv[:, :]).then_inc(w_in, 16)
            act.dma_start(consts[:, :], const_cols[:, :]).then_inc(tables_in, 16)
            for dst, src in ((wd_s, wd), (wuk_s, wuk), (wuv_s, wuv)):
                act.dma_start(dst, src[:, :]).then_inc(fold_w_in, 16)
            act.dma_start(wo_s[:, :], wo[:, :]).then_inc(const_in, 16)
            act.dma_start(w8_s[:, :], w8[:, :]).then_inc(const_in, 16)
            act.dma_start(bias_s[:, :], bias.broadcast_to([P, D])).then_inc(const_in, 16)
            act.dma_start(scales[:, 0:1], s_in.broadcast_to([P, 1])).then_inc(const_in, 16)
            act.dma_start(scales[:, 1:2], s_k.broadcast_to([P, 1])).then_inc(const_in, 16)

            act.wait_ge(fold_pe, 1)
            nc.scalar.copy(wkv_T, ps[:, 6, 0:D]).then_inc(fold_act, 1)
            act.wait_ge(fold_pe, 2)
            nc.scalar.copy(wdown_T, ps[0:DL, 7, 0:D]).then_inc(fold_act, 1)
            act.wait_ge(fold_pe, 3)
            nc.scalar.copy(wk_eff[:, :], ps[:, 6, 0:D]).then_inc(fold_act, 1)
            nc.scalar.copy(wv_eff[:, :], ps[:, 6, D:2 * D]).then_inc(fold_act, 1)

            def copy_v(c, bank_no):
                act.wait_ge(v_ps, c + 1)
                nc.scalar.copy(V[:, 4 * c:4 * c + 4, :, 0:HD],
                               ps[:, bank_no, :].rearrange("p (t h d) -> p t h d", t=4, h=H)).then_inc(v_sb, 1)

            for n, (kind, c) in enumerate(JOBS):
                cols = slice(c * CH, (c + 1) * CH)
                if kind == "T":
                    act.wait_ge(tr_ready, c + 1)
                    nc.scalar.copy(xnT[:, cols], ps[:, n % 8, :]).then_inc(xnT_ready, 1)
                elif kind == "q":
                    act.wait_ge(q_ps, c + 1)
                    nc.scalar.square(squares(Q, c), ps[:, n % 8, :])
                    nc.scalar.copy(qT[:, cols], ps[:, n % 8, :]).then_inc(q_sb, 1)
                elif kind == "k":
                    act.wait_ge(k_ps, c + 1)
                    nc.scalar.square(squares(K, c), ps[:, n % 8, :])
                    nc.scalar.copy(kT[:, cols], ps[:, n % 8, :]).then_inc(k_sb, 1)
                else:
                    copy_v(c, n % 8)
            for i, c in enumerate(LATE_V):
                copy_v(c, V_BANKS[i % 3])

            def finish_batch(b):
                for half in range(2):
                    act.wait_ge(ln2_ready, 2 * b + half + 1)
                    nc.scalar.mul(xs[:, halves[half]], xn2[:, halves[half]], rscales[:, 0:1]).then_inc(scaled, 1)
                for half in range(2):
                    act.wait_ge(xqT_ps, 2 * b + half + 1)
                    nc.scalar.copy(xqT[:, halves[half]], bank16(4 + half)).then_inc(xqT_ready, 1)
                for half in range(2):
                    act.wait_ge(y_ps, 2 * b + half + 1)
                    nc.scalar.mul(yb[:, halves[half]], bank(6 + half), oscale[:, 0:1]).then_inc(y_ready, 1)

            act.wait_ge(flag_ready, 1)
            bounded = act.value_load(flag[0:1, 0:1], min_val=0, max_val=1)
            with act.If(bounded > 0):
                act.sem_inc(scaled, 2 * (B - 1))
                def batch(b, first):
                    for hg in range(G):
                        for m in range(NB * HG):
                            kc, j = m // HG, m % HG
                            n = (b * G + hg) * NB * HG + m
                            if j == 0:
                                act.wait_ge(pv_done, (b * G + hg) * NB + kc + 1)
                            act.wait_ge(qk_done, n + 1)
                            act.wait_ge(diag_fixed, n + 1)
                            nc.scalar.activation(probs[:, m % (2 * HG), :], score[slot(hg, m, first=first)], ACT.Exp,
                                                 scale=SCALE).then_inc(exp_done, 1)

                batch(0, True)
                with act.Fori(1, B) as b:
                    batch(b, False)
            with act.Else():
                def heads(b):
                    with act.Fori(0, H) as h:
                        for t in range(NB):
                            act.wait_ge(g_max, (b * H + h) * NB + t + 1)
                            nc.scalar.activation(g_p, g_dec_s, ACT.Exp, bias=norms[:, 7:8]).then_inc(g_exp, 1)
                    for half in range(2):
                        act.wait_ge(g_otr, 2 * b + half + 1)
                        nc.scalar.copy(OT[:, halves[half]], bank(half)).then_inc(g_ot, 1)
                    act.wait_ge(g_ot, 2 * b + 2)
                    act.sem_inc(ot_ready, 1)

                with act.Fori(0, B - 1) as b:
                    heads(b)
                    finish_batch(b)
                heads(B - 1)
                act.sem_inc(ot_ready, 1)

            finish_batch(B - 1)

        @block.tensor
        def _(pe):
            pe.wait_ge(wkv_ready, 1)
            pe.wait_ge(tables_in, 16)
            nc.tensor.transpose(ps[:, 6, 0:D], wk_s, eye).then_inc(fold_pe, 1)
            pe.wait_ge(fold_act, 1)
            pe.wait_ge(fold_w_in, 48)
            nc.tensor.matmul(ps[0:DL, 7, 0:D], wd_s, wkv_T, start=True, stop=True).then_inc(fold_pe, 1)
            pe.wait_ge(fold_act, 2)
            nc.tensor.matmul(ps[:, 6, 0:D], wdown_T, wuk_s, start=True, stop=True)
            nc.tensor.matmul(ps[:, 6, D:2 * D], wdown_T, wuv_s, start=True, stop=True).then_inc(fold_pe, 1)
            pe.wait_ge(fold_act, 4)
            pe.wait_ge(wq_in, 16)

            def values(c, bank_no):
                for t in range(4):
                    last = nc.tensor.matmul(ps[:, bank_no, t * P:(t + 1) * P],
                                            xnT[:, c * CH + t * P:c * CH + (t + 1) * P], wv_eff[:, :],
                                            start=True, stop=True)
                last.then_inc(v_ps, 1)

            evacuated = {"T": xnT_ready, "q": q_sb, "k": k_sb, "v": v_sb}
            for n, (kind, c) in enumerate(JOBS):
                cols = slice(c * CH, (c + 1) * CH)
                if n >= 8:
                    k0, c0 = JOBS[n - 8]
                    pe.wait_ge(evacuated[k0], c0 + 1)
                if kind == "T":
                    pe.wait_ge(xn_ready, c + 1)
                    for t in range(4):
                        last = nc.tensor.transpose(ps[:, n % 8, t * P:(t + 1) * P], X[:, 4 * c + t, :], eye)
                    last.then_inc(tr_ready, 1)
                elif kind == "q":
                    pe.wait_ge(xnT_ready, c + 1)
                    nc.tensor.matmul(ps[:, n % 8, :], wq_s[:, :], xnT[:, cols], start=True, stop=True).then_inc(q_ps, 1)
                elif kind == "k":
                    nc.tensor.matmul(ps[:, n % 8, :], wk_eff[:, :], xnT[:, cols], start=True, stop=True).then_inc(k_ps, 1)
                else:
                    values(c, n % 8)

            pe.wait_ge(q_sb, NC)
            pe.wait_ge(k_sb, NC)
            pe.wait_ge(v_sb, LATE_V[0])
            pe.wait_ge(const_ready, 1)
            for which in range(2):
                for half in range(2):
                    for b in range(B):
                        last = nc.tensor.matmul(ps[32 * b:32 * b + 32, 2 * which + half, :], hsum[:, :],
                                                squares(which, 2 * b + half), start=True, stop=True)
            last.then_inc(norm_ps, 1)
            for i, c in enumerate(LATE_V):
                if i >= 3:
                    pe.wait_ge(v_sb, c - 2)
                values(c, V_BANKS[i % 3])
            pe.wait_ge(ok_ready, 1)
            nc.tensor.matmul(ps[0:1, 4, 0:1], norms[:, 6:7], ones[:, :], start=True, stop=True).then_inc(ok_ps, 1)

            def project(b, half, bank_no, last=False):
                pe.wait_ge(ot_ready, b + 1 + (half if last else 0))
                for t in range(4):
                    k = 4 * half + t
                    last = nc.tensor.matmul(ps[:, bank_no, t * P:(t + 1) * P], OT[:, k * P:(k + 1) * P], wo_s[:, :],
                                            start=True, stop=True)
                last.then_inc(proj_ps, 1)

            def transpose_xq(b, *banks):
                for half in range(2):
                    pe.wait_ge(xq_ready, 2 * b + half + 1)
                    for t in range(4):
                        k = 4 * half + t
                        last = nc.tensor.transpose(bank16(banks[half])[:, t * P:(t + 1) * P], xq[:, k * P:(k + 1) * P],
                                                   eye16[:, :])
                    last.then_inc(xqT_ps, 1)

            def multiply(b, *banks):
                for half in range(2):
                    pe.wait_ge(xqT_ready, 2 * b + half + 1)
                    for t in range(4):
                        k = 4 * half + t
                        last = nc.tensor.matmul(ps[:, banks[half], t * P:(t + 1) * P], xqT[:, k * P:(k + 1) * P],
                                                kq[:, :], start=True, stop=True)
                    last.then_inc(y_ps, 1)

            def tail(b, last=False):
                project(b, 0, 2, last)
                project(b, 1, 3, last)
                transpose_xq(b, 4, 5)
                multiply(b, 6, 7)

            pe.wait_ge(flag_ready, 1)
            bounded = pe.value_load(flag[0:1, 0:1], min_val=0, max_val=1)
            with pe.If(bounded > 0):
                def qk(u, j, kc, slot, own_bank):
                    keys = slice(kc * P, (kc + 1) * P)
                    own, other = kc * P // CH * CH, (1 - kc * P // CH) * CH
                    if own_bank:
                        pieces = [(own, kc * P, MINUS), (kc * P, own + CH, PLUS)]
                    else:
                        pieces = [(other, other + CH, PLUS if other else MINUS)]
                    for lo, hi, v in pieces:
                        if lo < hi:
                            ins = nc.tensor.matmul(slot[:, lo:hi], stage[0:KROWS, u, j, K, v, keys],
                                                   stage[0:KROWS, u, j, Q, v, lo:hi], start=True, stop=True)
                    ins.then_inc(edge_ready if own_bank else qk_done, 1)

                def weigh(b, hg, kc, half):
                    if half == 0:
                        tile = (b * G + hg) * NB + kc
                        pe.wait_ge(exp_done, (tile + 1) * HG)
                        if kc == 0:
                            pe.wait_ge(vb_in[hg], 16 * b + 16)
                    if kc == 0:
                        pe.wait_ge(pv_copied, 2 * (b * G + hg) + half + 1)
                    for j in range(HG):
                        last = nc.tensor.matmul(pv[32 * j:32 * j + VW, half * CH:(half + 1) * CH],
                                                Vb[:, kc, hg * HG + j, :],
                                                probs[:, (kc % 2) * HG + j, half * CH:(half + 1) * CH],
                                                start=kc == 0, stop=kc == NB - 1)
                    last.then_inc((pv_first, pv_done)[half], 1)

                def batch(b, first):
                    for hg in range(G):
                        u = hg % 2
                        if first and hg == 1:
                            pe.wait_ge(pads_in[1], 16)
                        if not (first and hg == 0):
                            pe.wait_ge(stage_in[u], FILL * (2 * b + hg // 2 + 1))
                        for m in range(NB * HG):
                            kc, j = m // HG, m % HG
                            n = (b * G + hg) * NB * HG + m
                            if (hg, m) in INSERTED and not first:
                                tail_item(b - 1, INSERTED.index((hg, m)), slot(hg, m, True), b)
                            if first:
                                if hg > 0 or m >= 3:
                                    pe.wait_ge(exp_done, hg * NB * HG + m - 2)
                            else:
                                free_slot(b, item(hg, m))
                            if first and hg == 0 and kc == 0:
                                if j >= 2:
                                    pe.wait_ge(late_k_in[j - 2], FILL // HG // 2)
                                pe.wait_ge(head_in[j], FILL // HG // (1 + (j >= 2)))
                                if j == HG - 1:
                                    pe.sem_inc(stage_in[0], FILL)
                            qk(u, j, kc, score[slot(hg, m, first=first)], True)
                            if j % 2 == 0:
                                tile = hg * NB + kc - (1 if j else 2)
                                if tile >= 0:
                                    weigh(b, tile // NB, tile % NB, 1 - j // 2)
                                elif not first:
                                    weigh(b - 1, G + tile // NB, tile % NB, 1 - j // 2)
                            qk(u, j, kc, score[slot(hg, m, first=first)], False)

                def free_slot(b, i):
                    if i < 3:
                        pe.wait_ge(exp_done, b * CHUNKS - 3 + i + 1)
                    elif ITEMS[i - 3][0] == "scores":
                        pe.wait_ge(exp_done, b * CHUNKS + ITEMS[i - 3][1] + 1)
                    else:
                        k = ITEMS[i - 3][1]
                        if k < 2:
                            pe.wait_ge(x1_ready, 2 * (b - 1) + k + 1)
                        else:
                            pe.wait_ge((xqT_ready, y_ready)[k - 2], 2 * b)

                def tail_item(last_b, k, slot_no, b):
                    free_slot(b, ITEMS.index(("tail", k)))
                    if k < 2:
                        project(last_b, k, 2 * slot_no)
                    elif k == 2:
                        transpose_xq(last_b, 2 * slot_no, 2 * slot_no + 1)
                    else:
                        multiply(last_b, 2 * slot_no, 2 * slot_no + 1)

                pe.sem_inc(pv_done, 2)
                pe.wait_ge(pv_clear, 1)
                pe.wait_ge(pads_in[0], 16)
                batch(0, True)
                pe.wait_ge(kq_ready, 1)
                pe.wait_ge(const_in, 16 * 5)
                with pe.Fori(1, B) as b:
                    batch(b, False)
                weigh(B - 1, G - 1, NB - 2, 1)
                weigh(B - 1, G - 1, NB - 1, 0)
                weigh(B - 1, G - 1, NB - 1, 1)
                for half in range(2):
                    pe.wait_ge(spread, half + 1)
                    nc.tensor.matmul(bank(half), same_head, split_s[:, halves[half]], start=True,
                                     stop=True).then_inc(spread_ps, 1)
            with pe.Else():
                pe.wait_ge(kq_ready, 1)
                pe.wait_ge(const_in, 16 * 5)
                def heads(b):
                    with pe.Fori(0, H) as h:
                        i = b * H + h
                        pe.wait_ge(g_in, 32 * (i + 1))
                        for t in range(NB):
                            n = i * NB + t
                            pe.wait_ge(g_scores_free, n + 1)
                            for half in range(2):
                                last = nc.tensor.matmul(ps[:, half, :], g_q[:, t * P:(t + 1) * P],
                                                        g_k[:, half * CH:(half + 1) * CH], start=True, stop=True)
                            last.then_inc(g_scores, 1)
                            pe.wait_ge(g_exp, n + 1)
                            for k in range(NB):
                                last = nc.tensor.transpose(ps_all[:, 2 * CH + k * P:2 * CH + (k + 1) * P],
                                                           g_p[:, k * P:(k + 1) * P], eye)
                            last.then_inc(g_tr, 1)
                            pe.wait_ge(g_pT, n + 1)
                            for k in range(NB):
                                last = nc.tensor.matmul(ps[:, 4, 0:VW], g_pT_s[:, k * P:(k + 1) * P],
                                                        V[:, bass.ds(b * NB + k, 1), bass.ds(h, 1), :],
                                                        start=k == 0, stop=k == NB - 1)
                            last.then_inc(g_o, 1)
                    pe.wait_ge(g_norm, (b + 1) * H * NB + 1)
                    for half in range(2):
                        for t in range(4):
                            k = 4 * half + t
                            last = nc.tensor.transpose(ps[:, half, t * P:(t + 1) * P], g_otok[:, k * D:(k + 1) * D], eye)
                        last.then_inc(g_otr, 1)

                with pe.Fori(0, B - 1) as b:
                    heads(b)
                    tail(b)
                heads(B - 1)

            tail(B - 1, True)

        @block.vector
        def _(dve):
            count = [0]

            def chain(ins):
                count[0] += 1
                ins.then_inc(dve_step, 1)
                dve.wait_ge(dve_step, count[0])

            def inverse_std(lo, n):
                var, y, y2 = rs[:, 0, lo:lo + n], rs[:, 1, lo:lo + n], rs[:, 2, lo:lo + n]
                chain(nc.vector.tensor_scalar(var, mv[:, lo:lo + n, 1], EPS, None, ALU.add))
                chain(nc.vector.tensor_scalar(y2.bitcast(I32), var.bitcast(I32), 1, None, ALU.logical_shift_right))
                chain(nc.vector.tensor_scalar(y.bitcast(I32), y2.bitcast(I32), -1.0, RSQRT_MAGIC, ALU.mult, ALU.add))
                for _ in range(3):
                    chain(nc.vector.tensor_tensor(y2, y, y, ALU.mult))
                    chain(nc.vector.scalar_tensor_tensor(out=y2, in0=y2, scalar=-0.5, in1=var, op0=ALU.mult, op1=ALU.mult))
                    chain(nc.vector.scalar_tensor_tensor(out=y, in0=y2, scalar=1.5, in1=y, op0=ALU.add, op1=ALU.mult))

            def token_stats(src, lo, n):
                for t in range(lo, lo + n):
                    last = nc.vector.bn_stats(stats[:, t, :], src[:, t, :])
                chain(last)
                for t in range(lo, lo + n):
                    last = nc.vector.bn_aggr(mv[:, t, :], stats[:, t, :])
                chain(last)
                inverse_std(lo, n)

            def to_fp8_grid(src, m):
                chain(nc.vector.tensor_scalar(m.bitcast(I32), src.bitcast(I32), 0x7F800000, None, ALU.bitwise_and))
                return nc.vector.tensor_scalar(m, m, 2.0 ** -6, 1.5 * 2.0 ** 20, ALU.max, ALU.mult)

            def overflow_to_nan(dst, r, tmp):
                chain(nc.vector.scalar_tensor_tensor(out=tmp, in0=r, scalar=NAN_SCALE, in1=r, op0=ALU.mult, op1=ALU.mult))
                return nc.vector.scalar_tensor_tensor(out=dst, in0=tmp, scalar=0.0, in1=r, op0=ALU.mult, op1=ALU.add)

            nc.vector.memset(V[:, :, :, HD:VW], 1.0).then_inc(v_ones, 1)
            nc.vector.memset(ones[:, :], 1.0)

            def norm_tiles(lo, n):
                for b in range(lo // NB, (lo + n) // NB):
                    dve.wait_ge(x_in[b], 16)
                token_stats(X, lo, n)
                if lo >= 2 * NB:
                    dve.sem_inc(stats_ready, 1)
                    n = NB
                for t in range(lo, lo + n):
                    last = nc.vector.tensor_scalar(X[:, t, :], X[:, t, :], mv[:, t, 0:1], rs[:, 1, t:t + 1],
                                                   ALU.subtract, ALU.mult)
                    if t % 4 == 3:
                        last.then_inc(xn_ready, 1)

            def split(src, a, v):
                s0 = split_s[:, :]
                out0, out1, out2 = [part(0, a, k, v) for k in range(PARTS)]
                chain(nc.vector.tensor_tensor(s0, src, decay[:, (a + v) % 2, :], ALU.mult))
                chain(nc.vector.tensor_copy(out0, s0))
                chain(nc.vector.tensor_tensor(s0, s0, out0, ALU.subtract))
                chain(nc.vector.tensor_copy(out1, s0))
                chain(nc.vector.tensor_tensor(out2, s0, out1, ALU.subtract))

            norm_tiles(0, NB)
            dve.wait_ge(tables_in, 16)
            nc.vector.tensor_copy(hsum[:, :], hsum_f).then_inc(const_ready, 1)

            norm_tiles(NB, NB)
            norm_tiles(2 * NB, 2 * NB)
            dve.wait_ge(decay_in, 16)
            dve.wait_ge(q_sb, 2)
            split(qT[:, 0:S], Q, PLUS)
            split(qT[:, 0:S], Q, MINUS)
            dve.sem_inc(q_parts, 1)
            dve.wait_ge(k_sb, 2)
            split(kT[:, 0:S], K, PLUS)
            dve.sem_inc(parts_ready, 1)

            dve.wait_ge(norm_ps, 1)
            for i in range(2):
                nc.vector.tensor_reduce(norms[:, i:i + 1], ps_all[:, i * S:(i + 1) * S], AX.X, ALU.max)
                nc.vector.tensor_reduce(norms[:, 2 + i:3 + i], ps_all[:, i * S:(i + 1) * S], AX.X, ALU.add)
            chain(nc.vector.tensor_reduce(norms[:, 5:6], wv_eff[:, :], AX.X, ALU.max, apply_absolute_value=True))
            nc.vector.tensor_scalar(norms[:, 0:1], norms[:, 0:1], norms[:, 1:2], NORM_LIMIT, ALU.mult, ALU.is_le)
            nc.vector.tensor_scalar(norms[:, 2:3], norms[:, 2:3], norms[:, 3:4], 3.0e38, ALU.add, ALU.is_le)
            chain(nc.vector.tensor_scalar(norms[:, 5:6], norms[:, 5:6], VALUE_BOUND / (D * 12.0), None, ALU.is_le))
            chain(nc.vector.tensor_tensor(norms[:, 0:1], norms[:, 0:1], norms[:, 2:3], ALU.mult))
            nc.vector.tensor_tensor(norms[:, 6:7], norms[:, 0:1], norms[:, 5:6], ALU.mult).then_inc(ok_ready, 1)
            dve.wait_ge(v_sb, NC)
            nc.vector.memset(pv, 0.0).then_inc(pv_clear, 1)
            dve.wait_ge(ok_ps, 1)
            nc.vector.tensor_scalar(flag[0:1, 0:1], ps[0:1, 4, 0:1], P - 0.5, None, ALU.is_ge).then_inc(flag_ready, 1)

            def prepare_weights(step):
                if step == 0:
                    dve.wait_ge(const_in, 16 * 5)
                    dve.wait_ge(dram_out, 16 * 3 * B)
                    chain(nc.vector.reciprocal(rscales[:, :], scales[:, :]))
                    nc.vector.tensor_copy(eye16[:, :], eye)
                elif step == 1:
                    chain(nc.vector.tensor_scalar(w8f, w8_s[:, :], rscales[:, 1:2], None, ALU.mult))
                    nc.vector.tensor_tensor(oscale[:, :], scales[:, 0:1], scales[:, 1:2], ALU.mult)
                elif step == 2:
                    chain(to_fp8_grid(w8f, w8m))
                elif step == 3:
                    chain(nc.vector.tensor_tensor(w8f, w8f, w8m, ALU.add))
                elif step == 4:
                    chain(nc.vector.tensor_tensor(w8f, w8f, w8m, ALU.subtract))
                else:
                    overflow_to_nan(kq[:, :], w8f, w8m).then_inc(kq_ready, 1)

            tail_count = [0]

            def own(ins, b):
                tail_count[0] += 1
                ins.then_inc(tail_step, 1)
                wait(dve, tail_step, TAIL_STEPS * b + tail_count[0])

            def residual(b, half, bank_no):
                if half == 0:
                    wait(dve, x2_in, 16 * b + 16)
                wait(dve, proj_ps, 2 * b + half + 1)
                cols = halves[half]
                nc.vector.tensor_tensor(X1[:, cols], bank(bank_no), X1[:, cols], ALU.add).then_inc(x1_ready, 1)

            def tile_stats(tiles):
                for t in tiles:
                    last = nc.vector.bn_stats(stats[:, t, :], X1[:, t * D:(t + 1) * D])
                return last

            def gather_stats():
                for t in range(NB):
                    last = nc.vector.bn_aggr(mv[:, t, :], stats[:, t, :])
                return last

            def inverse_std_step(i):
                var, y, y2 = [rs[:, k, 0:NB] for k in range(3)]
                if i == 0:
                    return nc.vector.tensor_scalar(var, mv[:, 0:NB, 1], EPS, None, ALU.add)
                if i == 1:
                    return nc.vector.tensor_scalar(y2.bitcast(I32), var.bitcast(I32), 1, None, ALU.logical_shift_right)
                if i == 2:
                    return nc.vector.tensor_scalar(y.bitcast(I32), y2.bitcast(I32), -1.0, RSQRT_MAGIC, ALU.mult, ALU.add)
                if i % 3 == 0:
                    return nc.vector.tensor_tensor(y2, y, y, ALU.mult)
                if i % 3 == 1:
                    return nc.vector.scalar_tensor_tensor(out=y2, in0=y2, scalar=-0.5, in1=var, op0=ALU.mult, op1=ALU.mult)
                return nc.vector.scalar_tensor_tensor(out=y, in0=y2, scalar=1.5, in1=y, op0=ALU.add, op1=ALU.mult)

            def normalise_tiles(tiles):
                for t in tiles:
                    last = nc.vector.tensor_scalar(xn2[:, t * D:(t + 1) * D], X1[:, t * D:(t + 1) * D], mv[:, t, 0:1],
                                                   rs[:, 1, t:t + 1], ALU.subtract, ALU.mult)
                return last

            def divide(half):
                return nc.vector.tensor_scalar(xs[:, halves[half]], xn2[:, halves[half]], rscales[:, 0:1], None, ALU.mult)

            def grid_step(b, half):
                x_h, m_h = xs[:, halves[half]], magic[:, halves[half]]
                own(nc.vector.tensor_scalar(m_h.bitcast(I32), x_h.bitcast(I32), 0x7F800000, None, ALU.bitwise_and), b)
                nc.vector.tensor_scalar(m_h, m_h, 2.0 ** -6, 1.5 * 2.0 ** 20, ALU.max, ALU.mult).then_inc(magic_ready, 1)

            def quantised(b, half, step):
                x_h, m_h = xs[:, halves[half]], magic[:, halves[half]]
                if step == 0:
                    wait(dve, rounded, 2 * b + half + 1)
                    own(nc.vector.scalar_tensor_tensor(out=m_h, in0=x_h, scalar=NAN_SCALE, in1=x_h, op0=ALU.mult,
                                                       op1=ALU.mult), b)
                else:
                    nc.vector.scalar_tensor_tensor(out=xq[:, halves[half]], in0=m_h, scalar=0.0, in1=x_h, op0=ALU.mult,
                                                   op1=ALU.add).then_inc(xq_ready, 1)

            def add_bias(half):
                y3 = yb[:, halves[half]].rearrange("p (t d) -> p t d", d=D)
                return nc.vector.tensor_tensor(y3, y3, bias_s[:, :].rearrange("p (o d) -> p o d", o=1)
                                               .broadcast_to([P, 4, D]), ALU.add)

            def result(half):
                cols = halves[half]
                nc.vector.tensor_tensor(X1[:, cols], X1[:, cols], yb[:, cols], ALU.add).then_inc(res_ready, 1)

            def tail_piece(b, c):
                if c not in PIECES:
                    return
                i = PIECES.index(c)
                if c == XQT_CHUNK:
                    for half in range(2):
                        wait(dve, xqT_ps, 2 * b + half + 1)
                        nc.vector.tensor_copy(xqT[:, halves[half]],
                                              bank16(2 * slot(*INSERTED[2], True) + half)).then_inc(xqT_ready, 1)
                elif c == Y_CHUNK:
                    for half in range(2):
                        wait(dve, y_ps, 2 * b + half + 1)
                        nc.vector.tensor_scalar(yb[:, halves[half]], bank(2 * slot(*INSERTED[3], True) + half),
                                                oscale[:, 0:1], None, ALU.mult).then_inc(y_ready, 1)
                elif i < 2:
                    residual(b, i, 2 * slot(*INSERTED[i], True))
                elif i == 2:
                    wait(dve, x1_ready, 2 * b + 2)
                    tile_stats((0, 1))
                elif i < 5:
                    tile_stats((2 * i - 4, 2 * i - 3))
                elif i == 5:
                    own(tile_stats((6, 7)), b)
                elif i == 6:
                    own(gather_stats(), b)
                elif i < 13:
                    for step in (2 * i - 14, 2 * i - 13):
                        own(inverse_std_step(step), b)
                elif i < 16:
                    normalise_tiles((2 * i - 26, 2 * i - 25))
                elif i == 16:
                    own(normalise_tiles((6, 7)), b)
                elif i < 19:
                    own(divide(i - 17), b)
                    grid_step(b, i - 17)
                elif 24 <= i < 28:
                    quantised(b, (i - 24) // 2, i % 2)
                elif c == Y_CHUNK + 2:
                    wait(dve, y_ready, 2 * b + 2)
                    add_bias(0)
                    own(add_bias(1), b)
                elif c == Y_CHUNK + 4:
                    result(0)
                elif c == Y_CHUNK + 6:
                    result(1)

            def tail(b):
                tail_count[0] = 0
                residual(b, 0, 2)
                residual(b, 1, 3)
                wait(dve, x1_ready, 2 * b + 2)
                own(tile_stats(range(NB)), b)
                own(gather_stats(), b)
                for step in range(12):
                    own(inverse_std_step(step), b)
                for half in range(2):
                    normalise_tiles(range(4 * half, 4 * half + 4)).then_inc(ln2_ready, 1)
                for half in range(2):
                    wait(dve, scaled, 2 * b + half + 1)
                    grid_step(b, half)
                x_h, m_h = xs[:, halves[1]], magic[:, halves[1]]
                wait(dve, magic_ready, 2 * b + 2)
                own(nc.vector.tensor_tensor(x_h, x_h, m_h, ALU.add), b)
                own(nc.vector.tensor_tensor(x_h, x_h, m_h, ALU.subtract), b)
                wait(dve, rounded, 2 * b + 1)
                dve.sem_inc(rounded, 1)
                for half in range(2):
                    quantised(b, half, 0)
                    quantised(b, half, 1)
                for half in range(2):
                    wait(dve, y_ready, 2 * b + half + 1)
                    own(add_bias(half), b)
                    result(half)
                pad_steps(b)

            def pad_steps(b):
                assert tail_count[0] <= TAIL_STEPS
                if tail_count[0] < TAIL_STEPS:
                    dve.sem_inc(tail_step, TAIL_STEPS - tail_count[0])
                tail_count[0] = 0

            dve.wait_ge(flag_ready, 1)
            bounded = dve.value_load(flag[0:1, 0:1], min_val=0, max_val=1)
            with dve.If(bounded > 0):
                chained = count[0]
                dve.sem_inc(pv_copied, 2)
                dve.sem_inc(ln2_ready, 2 * (B - 1))

                def copy_pv(group, half, first):
                    if half == 0:
                        dve.wait_ge(pv_first, NB * (group + 1))
                        if not first:
                            dve.wait_ge(sums_moved, 16 * HG * group)
                            dve.wait_ge(out_moved, 16 * HG * group)
                    else:
                        dve.wait_ge(pv_done, NB * (group + 1) + 2)
                    nc.vector.tensor_copy(pv_out[0:96 + VW, halves[half]],
                                          pv[0:96 + VW, halves[half]]).then_inc(pv_copied, 1)

                def invert_sums(b, half):
                    if half == 0:
                        dve.wait_ge(sums_moved, 16 * HG * G * (b + 1))
                    part = slice(half * (S // HD // 2), (half + 1) * (S // HD // 2))
                    nc.vector.reciprocal(rec[:, part], den[:, part]).then_inc(rec_ready, 1)

                def batch(b, first):
                    for hg in range(G):
                        for m in range(NB * HG):
                            kc, j = m // HG, m % HG
                            dve.wait_ge(edge_ready, (b * G + hg) * NB * HG + m + 1)
                            own = score[slot(hg, m, first=first)][:, kc * P:(kc + 1) * P]
                            nc.vector.tensor_tensor(own, own, fix, ALU.mult).then_inc(diag_fixed, 1)
                            if m in (4, 6) and not (first and hg == 0):
                                copy_pv(b * G + hg - 1, m // 2 - 2, first and hg == 1)
                            if hg == 0 and m in (14, 16) and not first:
                                invert_sums(b - 1, m // 2 - 7)
                            if first and hg == 1 and m % 2 == 0 and 8 <= m < 20:
                                prepare_weights((m - 8) // 2)
                            if hg > 0 and not first:
                                tail_piece(b - 1, (hg - 1) * NB * HG + m)
                    if not first:
                        pad_steps(b - 1)

                batch(0, True)
                with dve.Fori(1, B) as b:
                    batch(b, False)
                copy_pv(B * G - 1, 0, False)
                copy_pv(B * G - 1, 1, False)
                invert_sums(B - 1, 0)
                invert_sums(B - 1, 1)
                dve.wait_ge(rec_ready, 2 * B)
                dve.wait_ge(parts_ready, 2 * B)
                wide = split_s[:, :].rearrange("p (c t) -> p c t", c=HD)
                for half in range(2):
                    c4 = slice(4 * half, 4 * half + 4)
                    nc.vector.tensor_tensor(wide[:, c4, :],
                                            rec[:, :].rearrange("p (o t) -> p o t", o=1).broadcast_to([P, 4, S // HD]),
                                            place[:, c4].rearrange("p (c o) -> p c o", o=1)
                                            .broadcast_to([P, 4, S // HD]), ALU.mult).then_inc(spread, 1)
                dve.wait_ge(out_moved, 16 * HG * G * B)
                for half in range(2):
                    dve.wait_ge(spread_ps, half + 1)
                    nc.vector.tensor_tensor(OT[:, halves[half]], o_raw[:, halves[half]], bank(half),
                                            ALU.mult).then_inc(ot_ready, 1)
            with dve.Else():
                count[0] = chained
                for step in range(6):
                    prepare_weights(step)
                dve.sem_inc(g_scores_free, 1)
                dve.sem_inc(g_norm, 1)
                dve.wait_ge(g_table, 16)
                def heads(b):
                    with dve.Fori(0, H) as h:
                        for t in range(NB):
                            n = (b * H + h) * NB + t
                            done = 4 * n
                            dve.wait_ge(g_scores, n + 1)
                            nc.vector.tensor_scalar(g_clip, ps_all[:, 0:S], SCALE, -CLAMP, ALU.mult, ALU.max).then_inc(g_step, 1)
                            dve.wait_ge(g_step, done + 1)
                            dve.sem_inc(g_scores_free, 1)
                            u0 = S - P - t * P
                            nc.vector.scalar_tensor_tensor(out=g_dec_s, in0=g_clip, scalar=CLAMP,
                                                           in1=g_table_s[:, u0:u0 + S], op0=ALU.min,
                                                           op1=ALU.mult).then_inc(g_step, 1)
                            dve.wait_ge(g_step, done + 2)
                            nc.vector.tensor_reduce(norms[:, 6:7], g_dec_s, AX.X, ALU.max).then_inc(g_step, 1)
                            dve.wait_ge(g_step, done + 3)
                            nc.vector.tensor_scalar(norms[:, 7:8], norms[:, 6:7], -1.0, None, ALU.mult).then_inc(g_max, 1)
                            dve.wait_ge(g_tr, n + 1)
                            nc.vector.tensor_copy(g_pT_s, ps_all[:, 2 * CH:2 * CH + S]).then_inc(g_pT, 1)
                            dve.wait_ge(g_o, n + 1)
                            nc.vector.reciprocal(norms[:, 5:6], ps[:, 4, HD:VW]).then_inc(g_step, 1)
                            dve.wait_ge(g_step, done + 4)
                            nc.vector.tensor_scalar(g_otok[:, bass.ds(t * D + h * HD, HD)], ps[:, 4, 0:HD],
                                                    norms[:, 5:6], None, ALU.mult).then_inc(g_norm, 1)

                with dve.Fori(0, B - 1) as b:
                    heads(b)
                    tail(b)
                heads(B - 1)

            tail(B - 1)


_INS = ['L0_attn_x', 'L0_attn_Wq', 'L0_attn_Wk', 'L0_attn_Wv', 'L0_attn_Wo', 'L0_attn_W_down_kv', 'L0_attn_W_up_k',
        'L0_attn_W_up_v', 'L0_ffn_kernel', 'L0_ffn_input_scale', 'L0_ffn_kernel_scale', 'L0_ffn_bias']


def constants():
    import numpy as np
    c = 0.01 * 0.01
    i = np.arange(S, dtype=np.float64)
    rows = np.concatenate([np.exp(-c * i), np.exp(c * i)])[None, :]
    p = np.arange(P)[:, None]
    table = np.exp(-c * np.abs(p - np.arange(TABLE)[None, :] + S - P))
    key, query = p, np.arange(P)[None, :]
    fix = np.exp(-2 * c * np.maximum(key - query, 0))
    head_sum = (np.arange(P)[:, None] // HD == np.arange(32)[None, :]).astype(np.float64)
    same_head = (p // HD == query // HD).astype(np.float64)
    place = (p % HD == np.arange(HD)[None, :]).astype(np.float64)
    return {"decay_rows": rows, "decay_table": table, "const_cols": np.concatenate([np.eye(P), fix, head_sum, same_head, place], 1),
            "zeros": np.zeros((1, HG * 2 * S))}


def kernel(**inputs):
    import numpy as np
    import concourse.bacc as bacc
    from concourse.bass_utils import run_bass_kernel_spmd

    nc = bacc.Bacc("TRN2", target_bir_lowering=False, num_devices=1)
    arrays = {}
    for name in _INS:
        a = np.ascontiguousarray(inputs[name])
        if a.ndim == 3:
            a = a.reshape(B * S, D)
        if a.ndim == 1:
            a = a.reshape(1, -1)
        arrays[name] = a
    for name, a in constants().items():
        arrays[name] = np.ascontiguousarray(a.astype(np.float32))
    args = [nc.dram_tensor(n, a.shape, mybir.dt.from_np(a.dtype), kind="ExternalInput").ap() for n, a in arrays.items()]
    out = nc.dram_tensor("out", (B * S, D), F32, kind="ExternalOutput").ap()
    qt_dram = nc.dram_tensor("qt_dram", (P, B * S), F32, kind="Internal").ap()
    kt_dram = nc.dram_tensor("kt_dram", (P, B * S), F32, kind="Internal").ap()
    v_dram = nc.dram_tensor("v_dram", (P, NT * H * VW), F32, kind="Internal").ap()
    rec_dram = nc.dram_tensor("rec_dram", (H, S), F32, kind="Internal").ap()
    build(nc, *args, out, qt_dram, kt_dram, v_dram, rec_dram)
    r = run_bass_kernel_spmd(nc, [arrays], core_ids=[0])
    return r.results[0]["out"].reshape(B, S, D)
```
